# Optimizing a Trainium2 kernel written in Bass

```python
import numpy as np
import jax
import jax.numpy as jnp

def _softmax(x, axis=-1):
    return jax.nn.softmax(x, axis=axis)

def _gelu(x):
    return jax.nn.gelu(x, approximate=True)

def _silu(x):
    return jax.nn.silu(x)

def _sigmoid(x):
    return jax.nn.sigmoid(x)

def _layernorm(x, axis=-1, eps=1e-05):
    m = jnp.mean(x, axis=axis, keepdims=True)
    v = jnp.var(x, axis=axis, keepdims=True)
    return (x - m) / jnp.sqrt(v + eps)

def _scatter_add(tgt, idx, src, axis=0):
    return tgt.at[idx].add(src)

def _segment_sum(src, seg, n):
    return jax.ops.segment_sum(src, seg, n)
kernel_name = 'mk_adj_resnorm_d2_adj_r2_7d6f2f'

def setup_inputs(seed: int=0):
    np.random.seed(seed)
    _w = jnp.asarray

    def _rec_inputs():
        import jax
        import jax.numpy as jnp
        _gk = jax.random.key(seed)
        x = -0.0002928 + 1 * jax.random.normal(jax.random.fold_in(_gk, 1), (2048, 512), jnp.float32)
        _a = jax.random.bernoulli(jax.random.fold_in(_gk, 2), 0.000976562, (2048, 2048))
        _a = jnp.logical_or(_a, jnp.swapaxes(_a, -1, -2))
        _a = jnp.logical_or(_a, jnp.eye(2048, dtype=bool))
        _af = _a.astype(jnp.float32)
        adj = _af
        return (x, adj)
    x, adj = _rec_inputs()

    def _L0_gnn_setup():
        import jax, jax.numpy as jnp
        import numpy as np
        N = 2048
        D_IN = 512
        H = 16
        DH = D_IN // H
        ALPHA = 0.2
        MASK_VAL = -65500.0
        key = jax.random.key(seed)
        ks = jax.random.split(key, 7)
        x = jax.random.normal(ks[0], (N, D_IN), dtype=jnp.float32)
        adj = jax.random.randint(ks[1], (N, N), 0, 2).astype(jnp.float32)
        s = 1.0 / np.sqrt(D_IN)
        W_seq = jax.random.normal(ks[2], (D_IN, D_IN), dtype=jnp.float32) * s
        a1 = jax.random.normal(ks[3], (DH,), dtype=jnp.float32) / np.sqrt(DH)
        a2 = jax.random.normal(ks[4], (DH,), dtype=jnp.float32) / np.sqrt(DH)
        W_out = jax.random.normal(ks[5], (D_IN, D_IN), dtype=jnp.float32) * s
        b_out = jax.random.normal(ks[6], (D_IN,), dtype=jnp.float32) * 0.01
        return {'x': x, 'adj': adj, 'W_seq': W_seq, 'a1': a1, 'a2': a2, 'W_out': W_out, 'b_out': b_out}
    _L0_gnn_all = _L0_gnn_setup()
    _L0_gnn_in = {k: v for k, v in _L0_gnn_all.items() if k in ('W_seq', 'a1', 'a2', 'W_out', 'b_out')}
    del _L0_gnn_all

    def _L1_gnn_setup():
        import jax, jax.numpy as jnp
        import numpy as np
        ALPHA = 0.2
        NEG = -9000000000000000.0
        N, NFEAT, NHID, NHEADS = (2048, 512, 64, 8)
        EMB = NHID * NHEADS
        key = jax.random.key(seed)
        ks = jax.random.split(key, 16)
        x = jax.random.normal(ks[0], (N, NFEAT), dtype=jnp.float32)
        adj = (jax.random.uniform(ks[1], (N, N)) < 0.01).astype(jnp.float32)
        adj = jnp.maximum(adj, jnp.eye(N, dtype=jnp.float32))
        s = 0.05
        W = jax.random.normal(ks[2], (NHEADS, NFEAT, NHID), dtype=jnp.float32) * s
        a1 = jax.random.normal(ks[3], (NHEADS, NHID), dtype=jnp.float32) * s
        a2 = jax.random.normal(ks[4], (NHEADS, NHID), dtype=jnp.float32) * s
        W1 = jax.random.normal(ks[5], (EMB // 2, EMB), dtype=jnp.float32) * s
        b1 = jnp.zeros((EMB // 2,), dtype=jnp.float32)
        W2 = jax.random.normal(ks[6], (NFEAT // 4, EMB // 2), dtype=jnp.float32) * s
        b2 = jnp.zeros((NFEAT // 4,), dtype=jnp.float32)
        W3 = jax.random.normal(ks[7], (NFEAT // 2, NFEAT // 4), dtype=jnp.float32) * s
        b3 = jnp.zeros((NFEAT // 2,), dtype=jnp.float32)
        W4 = jax.random.normal(ks[8], (NFEAT, NFEAT // 2), dtype=jnp.float32) * s
        b4 = jnp.zeros((NFEAT,), dtype=jnp.float32)
        return {'x': x, 'adj': adj, 'W': W, 'a1': a1, 'a2': a2, 'W1': W1, 'b1': b1, 'W2': W2, 'b2': b2, 'W3': W3, 'b3': b3, 'W4': W4, 'b4': b4}
    _L1_gnn_all = _L1_gnn_setup()
    _L1_gnn_in = {k: v for k, v in _L1_gnn_all.items() if k in ('W', 'a1', 'a2', 'W1', 'b1', 'W2', 'b2', 'W3', 'b3', 'W4', 'b4')}
    del _L1_gnn_all
    return {'x': x, 'adj': adj, 'L0_gnn_W_seq': _L0_gnn_in['W_seq'], 'L0_gnn_a1': _L0_gnn_in['a1'], 'L0_gnn_a2': _L0_gnn_in['a2'], 'L0_gnn_W_out': _L0_gnn_in['W_out'], 'L0_gnn_b_out': _L0_gnn_in['b_out'], 'L1_gnn_W': _L1_gnn_in['W'], 'L1_gnn_a1': _L1_gnn_in['a1'], 'L1_gnn_a2': _L1_gnn_in['a2'], 'L1_gnn_W1': _L1_gnn_in['W1'], 'L1_gnn_b1': _L1_gnn_in['b1'], 'L1_gnn_W2': _L1_gnn_in['W2'], 'L1_gnn_b2': _L1_gnn_in['b2'], 'L1_gnn_W3': _L1_gnn_in['W3'], 'L1_gnn_b3': _L1_gnn_in['b3'], 'L1_gnn_W4': _L1_gnn_in['W4'], 'L1_gnn_b4': _L1_gnn_in['b4']}

def reference(x, adj, L0_gnn_W_seq, L0_gnn_a1, L0_gnn_a2, L0_gnn_W_out, L0_gnn_b_out, L1_gnn_W, L1_gnn_a1, L1_gnn_a2, L1_gnn_W1, L1_gnn_b1, L1_gnn_W2, L1_gnn_b2, L1_gnn_W3, L1_gnn_b3, L1_gnn_W4, L1_gnn_b4):
    import jax
    import jax.numpy as jnp

    def _L0_gnn_ref(x, adj, W_seq, a1, a2, W_out, b_out):
        import jax, jax.numpy as jnp
        import numpy as np
        N = 2048
        D_IN = 512
        H = 16
        DH = D_IN // H
        ALPHA = 0.2
        MASK_VAL = -65500.0
        seq = (x @ W_seq).reshape(N, H, DH)
        score1 = jnp.einsum('nhd,d->hn', seq, a1)
        score2 = jnp.einsum('nhd,d->hn', seq, a2)
        scores = score1[:, :, None] + score2[:, None, :]
        scores = jax.nn.leaky_relu(scores, negative_slope=ALPHA)
        scores = scores + (1.0 - adj)[None, :, :] * MASK_VAL
        attn = jax.nn.softmax(scores, axis=-1)
        hidden = jnp.einsum('hij,jhd->ihd', attn, seq).reshape(N, D_IN)
        hidden = hidden @ W_out + b_out
        return jax.nn.elu(hidden)

    def _L1_gnn_ref(x, adj, W, a1, a2, W1, b1, W2, b2, W3, b3, W4, b4):
        import jax, jax.numpy as jnp
        import numpy as np
        ALPHA = 0.2
        NEG = -9000000000000000.0
        N, NFEAT, NHID, NHEADS = (2048, 512, 64, 8)
        EMB = NHID * NHEADS
        Wh = jnp.einsum('nf,hfd->hnd', x, W)
        e_src = jnp.einsum('hnd,hd->hn', Wh, a1)
        e_dst = jnp.einsum('hnd,hd->hn', Wh, a2)
        e = jax.nn.leaky_relu(e_src[:, :, None] + e_dst[:, None, :], ALPHA)
        e = jnp.where(adj[None] > 0, e, NEG)
        att = jax.nn.softmax(e, axis=-1)
        h = jnp.einsum('hnm,hmd->hnd', att, Wh)
        h = jax.nn.elu(h)
        enc = jnp.transpose(h, (1, 0, 2)).reshape(x.shape[0], -1)
        out = jax.nn.relu(enc @ W1.T + b1)
        out = jax.nn.relu(out @ W2.T + b2)
        out = jax.nn.relu(out @ W3.T + b3)
        out = out @ W4.T + b4
        return out
    x = _layernorm(x + _L0_gnn_ref(x, adj, L0_gnn_W_seq, L0_gnn_a1, L0_gnn_a2, L0_gnn_W_out, L0_gnn_b_out), axis=-1)
    x = _layernorm(x + _L1_gnn_ref(x, adj, L1_gnn_W, L1_gnn_a1, L1_gnn_a2, L1_gnn_W1, L1_gnn_b1, L1_gnn_W2, L1_gnn_b2, L1_gnn_W3, L1_gnn_b3, L1_gnn_W4, L1_gnn_b4), axis=-1)
    return x

_drawn_inputs = setup_inputs


def setup_inputs(seed=0):
    import zlib

    import numpy as np

    out = dict(_drawn_inputs(seed))
    spreads = {'L1_gnn_b1': (0.0, 0.67),
     'L1_gnn_b2': (0.0, 0.347),
     'L1_gnn_b3': (0.0, 0.1),
     'L1_gnn_b4': (0.0, 0.1)}
    factors = {'L0_gnn_b_out': 6.994, 'L1_gnn_a1': 23.466, 'L1_gnn_a2': 3.733}
    for name, (base, spread) in spreads.items():
        noise = np.random.default_rng([zlib.crc32(name.encode()), seed]).standard_normal(out[name].shape)
        drawn = base * np.exp(spread * noise) if base else spread * noise
        out[name] = jnp.asarray(drawn.astype(out[name].dtype))
    for name, factor in factors.items():
        out[name] = (out[name] * factor).astype(out[name].dtype)
    return out
```

```python
from contextlib import ExitStack

import concourse.bass as bass
from concourse import mybir

ds = bass.ds

P = 128
N = 2048
D = 512
T = N // P
KT = D // P
PARTS = 3
UNITS = 16
MASK_SLOTS = 8
STEP_SLOTS = 4
AHEAD = 3
BANKS = 8
BIG = 2.0 ** 80
TIE = 60.0
ONES8 = 0x38383838
LIFT = 64.0
EPS = 1e-5


class Layer:
    def __init__(self, name, heads, vector_tiles):
        self.name = name
        self.H = heads
        self.DH = D // heads
        self.C = self.DH + 1
        self.W = heads * N // UNITS
        self.NI = self.W // P
        self.per_bank = self.NI // BANKS
        self.UH = UNITS // heads
        self.TILE = 2 * PARTS * self.C
        self.vector_tiles = vector_tiles


def gat_kernel(nc, xT, x, adjT, w_seq, a1_0, a2_0, w_out, b_out, w_heads, a1_1, a2_1,
               w1T, b1, w2T, b2, w3T, b3, w4T, b4, out, packs, rows, x1_keep):
    dt = mybir.dt
    ALU = mybir.AluOpType
    ACT = mybir.ActivationFunctionType
    X = mybir.AxisListType.X
    f32, bf16, f8, u32 = dt.float32, dt.bfloat16, dt.float8e4, dt.uint32
    RMAX = bass.bass_isa.ReduceOp.max

    L0 = Layer("l0", 16, (5, 11))
    L1 = Layer("l1", 8, ())
    LAYERS = (L0, L1)

    ctx = ExitStack()
    with ctx:
        def sb(name, shape, dtype):
            return ctx.enter_context(nc.sbuf_tensor(name, shape, dtype))

        def sem(name):
            return ctx.enter_context(nc.semaphore(name))

        adj8 = sb("adj8", [P, T, N], f8)
        feat = sb("feat", [P, KT * N], f32)
        featT = feat[:, :].rearrange("p (k n) -> p k n", k=KT)
        hid = feat[:, :].rearrange("p (t d) -> p t d", t=T)
        w_proj = sb("w_proj", [P, KT, D], f32)
        w_out_sb = sb("w_out_sb", [P, KT, D], f32)
        w1_sb = sb("w1_sb", [P, 4, 256], f32)
        w2_sb = sb("w2_sb", [P, 2, 128], f32)
        w3_sb = sb("w3_sb", [P, 256], f32)
        w4_sb = sb("w4_sb", [P, 2, D], f32)
        b_out_sb = sb("b_out_sb", [P, D], f32)
        b4_sb = sb("b4_sb", [P, D], f32)
        b1_sb = sb("b1_sb", [P, 2], f32)
        b2_sb = sb("b2_sb", [P, 1], f32)
        b3_sb = sb("b3_sb", [P, 2], f32)
        ident = sb("ident", [P, P], f32)
        a_bc = sb("a_bc", [P, 2, D], f32)
        wa = sb("wa", [P, KT, 32], f32)
        ab = sb("ab", [P, T * 32], f32)
        tmp = sb("tmp", [P, T * 16], f32)
        tmp2 = sb("tmp2", [P, T * 16], f32)
        a_ht = sb("a_ht", [P, T * 16], f32)
        a_rows_sb = sb("a_rows_sb", [P, 2, P], f32)
        bmax_part = sb("bmax_part", [P, 16], f32)
        bmax = sb("bmax", [P, 16], f32)
        BB = sb("BB", [P, T * 16 * 2], f32)
        ww = sb("ww", [P, T * 16 * 2], f32)
        thr = sb("thr", [P, T * 16 * 2], f32)
        thr_unit = sb("thr_unit", [P, 2, 2, T], f32)
        steps = sb("steps", [P, STEP_SLOTS, N], f8)
        step_v = sb("step_v", [P, N], f8)
        num = sb("num", [P, 2, 1056], f32)
        den = sb("den", [P, 544], f32)
        rec = sb("rec", [P, T], f32)
        stats = sb("stats", [P, 2, 6], f32)
        mv = sb("mv", [P, T, 2], f32)
        mv_tile = sb("mv_tile", [P, 2, 2], f32)
        std = sb("std", [P, T], f32)
        rstd = sb("rstd", [P, T], f32)
        big = sb("big", [P, T * D], f32)
        resid = big[:, :].rearrange("p (t d) -> p t d", t=T)
        rows_sb = sb("rows_sb", [P, 2 * N], f32)
        PACK = T * L1.TILE
        pack_sb = sb("pack_sb", [P, 2 * PACK], bf16)
        spare = pack_sb[:, :].bitcast(f32)
        adj_in = spare[:, 0:2 * N].rearrange("p (s n) -> p s n", s=2)
        yb = spare[:, 0:2 * D].rearrange("p (s d) -> p s d", s=2)
        eb = spare[:, 2 * D:4 * D].rearrange("p (s d) -> p s d", s=2)
        hT = spare[:, 4 * D:6 * D].rearrange("p (s k n) -> p s k n", s=2, k=KT)
        h1T = spare[:, 4 * D:6 * D].rearrange("p (f n) -> p f n", f=2)
        h2T = spare[:, 6 * D:7 * D]
        h3T = spare[:, 7 * D:9 * D].rearrange("p (f n) -> p f n", f=2)
        encT = rows_sb[:, :].rearrange("p (s k n) -> p s k n", s=2, k=KT)

        psum = ctx.enter_context(nc.psum_tensor("psum", [P, BANKS, 512], f32))

        x_in = sem("x_in")
        w_in = sem("w_in")
        a_in = sem("a_in")
        const_in = sem("const_in")
        adj_in_done = [sem(f"adj_in_done_{i}") for i in range(2)]
        adj_made = sem("adj_made")
        ident_step = sem("ident_step")
        dve_order = sem("dve_order")
        pe_gate = sem("pe_gate")
        act_gate = sem("act_gate")
        sp_gate = sem("sp_gate")
        dve_gate = sem("dve_gate")
        S = {}
        for lay in LAYERS:
            for what in ("wa_made", "ab_ready", "bmax_part_made", "bmax_made", "exps_ready", "exps_made",
                         "a_ht_made", "a_rows_ready", "a_rows_copied", "a_rows_out",
                         "v_ready", "v_copied", "x_made", "hi_made", "r_made", "mid_made", "lo_made",
                         "packs_out0", "packs_out1", "pack_loaded0", "pack_loaded1",
                         "row_loaded0", "row_loaded1", "thr_made", "step_made",
                         "compare_made", "masks_made", "mask_slots_free", "acc_ready", "acc_free",
                         "norm_order", "hid_made"):
                S[lay.name, what] = sem(f"{lay.name}_{what}")
        resid_in = [sem(f"resid_in_{i}") for i in range(2)]
        t_ready = sem("t_ready")
        t_copied = sem("t_copied")
        o_ready = sem("o_ready")
        y_made = sem("y_made")
        m_made = sem("m_made")
        e_made = sem("e_made")
        z_order = sem("z_order")
        var_made = sem("var_made")
        std_made = sem("std_made")
        x1_made = sem("x1_made")
        x1T_ready = sem("x1T_ready")
        x1T_copied = sem("x1T_copied")
        x1_out = sem("x1_out")
        x1_back = [sem(f"x1_back_{i}") for i in range(2)]
        min_made = sem("min_made")
        exp_made = sem("exp_made")
        enc_made = sem("enc_made")
        e_ready = sem("e_ready")
        e_copied = sem("e_copied")
        h_ready = sem("h_ready")
        h_made = sem("h_made")
        f_ready = sem("f_ready")
        f_read = sem("f_read")
        g_order = sem("g_order")
        var2_made = sem("var2_made")
        std2_made = sem("std2_made")
        out_made = sem("out_made")
        out_done = sem("out_done")

        def bb(lay):
            return BB[:, 0:T * lay.H * 2].rearrange("p (t h m) -> p t h m", t=T, m=2)

        def wv(lay):
            return ww[:, 0:T * lay.H * 2].rearrange("p (h t m) -> p h t m", t=T, m=2)

        def thrv(lay):
            return thr[:, 0:T * lay.H * 2].rearrange("p (h m t) -> p h m t", t=T, m=2)

        def aht(lay):
            return a_ht[:, 0:T * lay.H].rearrange("p (h t) -> p h t", t=T)

        def abv(lay):
            return ab[:, 0:T * 2 * lay.H].rearrange("p (t c) -> p t c", t=T)

        def xbuf(lay, s):
            n = lay.H * 2 * lay.C
            return rows_sb[:, s * n:(s + 1) * n].rearrange("p (h m c) -> p h m c", h=lay.H, m=2)

        def vbuf(lay, s):
            n = lay.H * lay.C
            o = 4 * n + s * n
            return rows_sb[:, o:o + n].rearrange("p (h c) -> p h c", h=lay.H)

        def staged(lay, g):
            n = lay.H * 2 * lay.TILE
            return big[:, :].bitcast(bf16)[:, g * n:(g + 1) * n].rearrange(
                "p (h t m r c) -> p h t m r c", h=lay.H, t=2, m=2, r=PARTS)

        def masks(lay, slot, m):
            n = lay.W
            o = (slot * 2 + m) * n
            return big[:, :].bitcast(f8)[:, o:o + n]

        def pack(lay, s):
            return pack_sb[:, s * PACK:s * PACK + T * lay.TILE].rearrange(
                "p (t m c) -> p t m c", t=T, m=2)

        def row(lay, s):
            return rows_sb[:, s * N:s * N + lay.W]

        def bank_out(lay, it, m):
            c = PARTS * lay.C
            o = ((it % lay.per_bank) * 2 + m) * c
            return psum[:, it // lay.per_bank, o:o + c]

        def cut(lay, q, s):
            return slice(0, T) if lay.UH == 1 else slice(s * lay.NI, (s + 1) * lay.NI)

        def head(lay, q, s):
            return 2 * q + s if lay.UH == 1 else q

        def pack_dram(lay):
            n = lay.H * P * T * lay.TILE
            return packs[0:n].rearrange("(h p c) -> h p c", h=lay.H, p=P)

        VOUT = 4

        block = ctx.enter_context(nc.Block())

        @block.sync
        def _(sp):
            def load_packs(lay):
                pd = pack_dram(lay)

                def unit(q, s):
                    sp.dma_start(pack_sb[:, s * PACK:s * PACK + T * lay.TILE],
                                 pd[ds(head(lay, q, s), 1), :, :].rearrange("o p c -> p (o c)"))\
                        .then_inc(S[lay.name, f"pack_loaded{s}"], 16)
                    sp.dma_start(row(lay, s),
                                 rows[ds(2 * q + s, 1), 0:lay.W].partition_broadcast(P)
                                 if lay is L0 else
                                 rows_half[ds(2 * q + s, 1), :].partition_broadcast(P))\
                        .then_inc(S[lay.name, f"row_loaded{s}"], 16)

                rows_half = rows[0:8, :].rearrange("h (g n) -> (h g) n", g=2)
                for i in range(2):
                    sp.wait_ge(S[lay.name, f"packs_out{i}"], 16 * (T // 4))
                sp.wait_ge(S[lay.name, "a_rows_out"], 16)
                sp.wait_ge(S[lay.name, "lo_made"], T)
                if lay is L0:
                    sp.wait_ge(adj_made, T)
                for s in range(2):
                    unit(0, s)
                with sp.Fori(1, UNITS // 2, 1) as q:
                    for s in range(2):
                        sp.wait_ge(S[lay.name, "acc_ready"], 16 * q + (BANKS * s - BANKS))
                        sp.sem_inc(sp_gate, 1)
                        sp.wait_ge(S[lay.name, "masks_made"], 32 * q + (T * s - T + STEP_SLOTS))
                        unit(q, s)

            def store_packs(lay, g):
                sp.wait_ge(S[lay.name, "lo_made"], 2 * g + 2)
                n = 2 * lay.TILE
                sp.dma_start(pack_dram(lay)[:, :, g * n:(g + 1) * n].rearrange("h p c -> p h c"),
                             staged(lay, g % 2).rearrange("p h t m r c -> p h (t m r c)"))\
                    .then_inc(S[lay.name, f"packs_out{g % 2}"], 16)

            def store_rows(lay):
                n = lay.H * T // P
                sp.wait_ge(S[lay.name, "a_rows_copied"], 1)
                sp.dma_start(rows[0:lay.H, :].rearrange("h (t n) -> (h t) n", t=T)
                             .rearrange("(c q) n -> q c n", c=n),
                             a_rows_sb[:, 0:n, :]).then_inc(S[lay.name, "a_rows_out"], 16)

            sp.dma_start(w_proj[:, :, :], w_seq.rearrange("(k p) n -> p k n", p=P)).then_inc(w_in, 16)
            sp.dma_start(a_bc[:, 0, 0:L0.DH], a1_0.partition_broadcast(P)).then_inc(a_in, 16)
            sp.dma_start(a_bc[:, 1, 0:L0.DH], a2_0.partition_broadcast(P)).then_inc(a_in, 16)
            for k in range(KT):
                sp.dma_start(featT[:, k, :], xT[k * P:(k + 1) * P, :]).then_inc(x_in, 16)
            for t in range(2):
                sp.dma_start(adj_in[:, t, :], adjT[t * P:(t + 1) * P, :]).then_inc(adj_in_done[t % 2], 16)
            store_rows(L0)
            for dst, src in ((w_out_sb[:, :, :], w_out.rearrange("(k p) n -> p k n", p=P)),
                             (w1_sb[:, :, :], w1T.rearrange("(k p) n -> p k n", p=P)),
                             (w2_sb[:, :, :], w2T.rearrange("(k p) n -> p k n", p=P)),
                             (w3_sb[:, :], w3T),
                             (w4_sb[:, :, :], w4T.rearrange("(k p) n -> p k n", p=P)),
                             (b_out_sb[:, :], b_out.partition_broadcast(P)),
                             (b4_sb[:, :], b4.partition_broadcast(P)),
                             (b1_sb[:, :], b1), (b2_sb[:, :], b2), (b3_sb[:, :], b3)):
                sp.dma_start(dst, src).then_inc(const_in, 16)
            for t in range(2, T):
                if t >= 4 and t % 2 == 0:
                    store_packs(L0, t // 2 - 2)
                sp.wait_ge(adj_made, t - 1)
                sp.dma_start(adj_in[:, t % 2, :], adjT[t * P:(t + 1) * P, :]).then_inc(adj_in_done[t % 2], 16)
            for g in range(T // 2 - 2, T // 2):
                store_packs(L0, g)
            load_packs(L0)

            sp.dma_start(w_proj[:, :, :], w_heads.rearrange("(k p) n -> p k n", p=P)).then_inc(w_in, 16)
            sp.dma_start(a_bc[:, 0, :], a1_1.partition_broadcast(P)).then_inc(a_in, 16)
            sp.dma_start(a_bc[:, 1, :], a2_1.partition_broadcast(P)).then_inc(a_in, 16)

            sp.wait_ge(S["l0", "acc_ready"], BANKS * UNITS)
            for t in range(T):
                if t >= 2:
                    sp.wait_ge(resid_in[t % 2], 16 * (t // 2))
                sp.dma_start(resid[:, t, :], x[t * P:(t + 1) * P, :]).then_inc(resid_in[t % 2], 16)
            with sp.Fori(0, T // 2, 1) as q:
                for s in range(2):
                    sp.wait_ge(x1_made, 2 * q + (s + 1))
                    sp.dma_start(x1_keep[ds(2 * q + s, 1), :, :].rearrange("o p d -> p (o d)"),
                                 resid[:, ds(2 * q + s, 1), :].rearrange("p o d -> p (o d)"))\
                        .then_inc(x1_out, 16)

            store_rows(L1)
            for g in range(T // 2):
                store_packs(L1, g)
            load_packs(L1)
            sp.wait_ge(S["l1", "acc_ready"], BANKS * UNITS)
            for t in range(T):
                if t >= 2:
                    sp.wait_ge(x1_back[t % 2], 16 * (t // 2))
                sp.dma_start(resid[:, t, :], x1_keep[t, :, :]).then_inc(x1_back[t % 2], 16)
            with sp.Fori(0, T // 2, 1) as q:
                for s in range(2):
                    sp.wait_ge(out_made, 2 * q + (s + 1))
                    sp.dma_start(out[ds(2 * q + s, 1), :, :].rearrange("o p d -> p (o d)"),
                                 resid[:, ds(2 * q + s, 1), :].rearrange("p o d -> p (o d)"))\
                        .then_inc(out_done, 16)
            sp.wait_ge(out_done, 16 * T)

        @block.gpsimd
        def _(pool):
            nc.gpsimd.memset(ident[:, :], 0.0).then_inc(ident_step, 1)
            pool.wait_ge(ident_step, 1)
            nc.gpsimd.affine_select(out=ident[:, :], in_=ident[:, :], compare_op=ALU.not_equal, fill=1.0,
                                    base=0, pattern=[[-1, P]], channel_multiplier=1)\
                .then_inc(ident_step, 1)
            for lay in LAYERS:
                pool.wait_ge(S[lay.name, "bmax_part_made"], 1)
                nc.gpsimd.partition_all_reduce(bmax[:, 0:lay.H], bmax_part[:, 0:lay.H], P, RMAX)\
                    .then_inc(S[lay.name, "bmax_made"], 1)

        @block.scalar
        def _(act):
            def prep(lay):
                n = lay.name
                if lay is L1:
                    act.wait_ge(x1_out, 16 * T)
                act.wait_ge(S[n, "exps_ready"], 4)
                nc.scalar.activation(BB[:, 0:T * lay.H * 2], BB[:, 0:T * lay.H * 2], ACT.Exp)\
                    .then_inc(S[n, "exps_made"], 1)
                nc.scalar.activation(ww[:, 0:T * lay.H * 2], ww[:, 0:T * lay.H * 2], ACT.Exp)\
                    .then_inc(S[n, "exps_made"], 1)

                def copy_v(t):
                    act.wait_ge(S[n, "v_ready"], t + 1)
                    if t >= 2:
                        act.wait_ge(S[n, "x_made"], t - 1)
                    nc.scalar.activation(vbuf(lay, t % 2)[:, :, 0:lay.DH],
                                         psum[:, t % VOUT, :].rearrange("p (h d) -> p h d", h=lay.H),
                                         ACT.Copy).then_inc(S[n, "v_copied"], 1)

                copy_v(0)
                for t in range(T):
                    dst = staged(lay, t // 2 % 2)
                    act.wait_ge(S[n, "x_made"], t + 1)
                    if t % 2 == 0 and t >= 4:
                        act.wait_ge(S[n, f"packs_out{t // 2 % 2}"], 16 * (t // 4))
                    nc.scalar.activation(dst[:, :, t % 2, :, 0, :], xbuf(lay, t % 2), ACT.Copy)\
                        .then_inc(S[n, "hi_made"], 1)
                    if t + 1 < T:
                        copy_v(t + 1)
                    act.wait_ge(S[n, "r_made"], t + 1)
                    nc.scalar.activation(dst[:, :, t % 2, :, 1, :], xbuf(lay, t % 2), ACT.Copy)\
                        .then_inc(S[n, "mid_made"], 1)

            def compares(lay):
                n = lay.name
                mine = [t for t in range(T) if t not in lay.vector_tiles]
                with act.Fori(0, UNITS // 2, 1) as q:
                    for s in range(2):
                        act.wait_ge(S[n, f"row_loaded{s}"], 16 * q + 16)
                        act.wait_ge(S[n, "thr_made"], 2 * q + (s + 1))
                        for c, t in enumerate(mine):
                            before = mine[c - STEP_SLOTS]
                            back = 0 if c >= STEP_SLOTS else T
                            act.wait_ge(S[n, "masks_made"],
                                        32 * q + (T * s - back + before + 1 + T + STEP_SLOTS))
                            act.sem_inc(act_gate, 1)
                            nc.scalar.activation(steps[:, (c + s * len(mine)) % STEP_SLOTS, 0:lay.W],
                                                 row(lay, s), ACT.Sigmoid,
                                                 bias=thr_unit[:, s, 0, t:t + 1], scale=BIG, saturate=False)\
                                .then_inc(S[n, "step_made"], 1)

            prep(L0)
            compares(L0)

            def exp_of(q, s):
                act.wait_ge(m_made, 2 * q + (s + 1))
                nc.scalar.activation(eb[:, s, :], eb[:, s, :], ACT.Exp).then_inc(e_made, 1)

            def copy_hT(q, s):
                act.wait_ge(t_ready, 2 * q + (s + 1))
                nc.scalar.activation(hT[:, s, :, :],
                                     psum[:, s, :].rearrange("p (k n) -> p k n", k=KT), ACT.Copy)\
                    .then_inc(t_copied, 1)

            copy_hT(0, 0)
            with act.Fori(0, T // 2 - 1, 1) as q:
                copy_hT(q, 1)
                exp_of(q, 0)
                copy_hT(q + 1, 0)
                exp_of(q, 1)
            copy_hT(T // 2 - 1, 1)
            exp_of(T // 2 - 1, 0)
            exp_of(T // 2 - 1, 1)
            act.wait_ge(var_made, 1)
            nc.scalar.activation(std[:, :], std[:, :], ACT.Sqrt).then_inc(std_made, 1)
            with act.Fori(0, T // 2, 1) as q:
                for s in range(2):
                    act.wait_ge(x1T_ready, 2 * q + (s + 1))
                    nc.scalar.activation(featT[:, :, ds(P * (2 * q + s), P)],
                                         psum[:, 4 + s, :].rearrange("p (k n) -> p k n", k=KT), ACT.Copy)\
                        .then_inc(x1T_copied, 1)

            prep(L1)
            compares(L1)

            def enc_side(c):
                for t in range(4 * c, 4 * c + 4):
                    act.wait_ge(min_made, t + 1)
                    nc.scalar.activation(eb[:, t % 2, :], eb[:, t % 2, :], ACT.Exp).then_inc(exp_made, 1)
                    if t >= 1 and t - 1 >= 4 * c:
                        act.wait_ge(e_ready, t)
                        nc.scalar.activation(encT[:, c % 2, :, (t - 1) % 4 * P:((t - 1) % 4 + 1) * P],
                                             psum[:, (t - 1) % 2, :].rearrange("p (k n) -> p k n", k=KT),
                                             ACT.Copy).then_inc(e_copied, 1)
                t = 4 * c + 3
                act.wait_ge(e_ready, t + 1)
                nc.scalar.activation(encT[:, c % 2, :, 3 * P:4 * P],
                                     psum[:, t % 2, :].rearrange("p (k n) -> p k n", k=KT),
                                     ACT.Copy).then_inc(e_copied, 1)

            enc_side(0)
            for c in range(4):
                if c < 3:
                    enc_side(c + 1)
                for f in range(2):
                    act.wait_ge(h_ready, 5 * c + f + 1)
                    nc.scalar.activation(h1T[:, f, :], psum[:, 2 + f, :], ACT.Relu, bias=b1_sb[:, f:f + 1])\
                        .then_inc(h_made, 1)
                act.wait_ge(h_ready, 5 * c + 3)
                nc.scalar.activation(h2T, psum[:, 4, :], ACT.Relu, bias=b2_sb[:, 0:1]).then_inc(h_made, 1)
                for f in range(2):
                    act.wait_ge(h_ready, 5 * c + 4 + f)
                    if c >= 1 and f == 0:
                        act.wait_ge(f_ready, 4 * c)
                    nc.scalar.activation(h3T[:, f, :], psum[:, 5 + f, :], ACT.Relu, bias=b3_sb[:, f:f + 1])\
                        .then_inc(h_made, 1)
            act.wait_ge(var2_made, 1)
            nc.scalar.activation(std[:, :], std[:, :], ACT.Sqrt).then_inc(std2_made, 1)

        @block.vector
        def _(dve):
            ordered = [0]

            def link(ins):
                ordered[0] += 1
                ins.then_inc(dve_order, 1)
                dve.wait_ge(dve_order, ordered[0])

            def scores_of_weights(lay, i):
                dve.wait_ge(w_in, 16 * (i + 1))
                dve.wait_ge(a_in, 32 * (i + 1))
                length = lay.DH if lay is L0 else D
                groups = KT * D // length
                prod = rows_sb[:, 0:KT * D]
                for v in range(2):
                    link(nc.vector.tensor_tensor(
                        prod.rearrange("p (g l) -> p g l", l=length),
                        w_proj[:, :, :].rearrange("p k n -> p (k n)").rearrange("p (g l) -> p g l", l=length),
                        a_bc[:, v, 0:length].unsqueeze(1).broadcast_to([P, groups, length]), ALU.mult))
                    last = nc.vector.tensor_reduce(
                        wa[:, :, v * lay.H:(v + 1) * lay.H],
                        prod.rearrange("p (k h d) -> p k h d", k=KT, d=lay.DH), X, ALU.add)
                    if v == 0:
                        link(last)
                    else:
                        last.then_inc(S[lay.name, "wa_made"], 1)

            def factors(lay):
                n, H = lay.name, lay.H
                dve.wait_ge(S[n, "ab_ready"], 1)
                link(nc.vector.tensor_copy(ab[:, 0:T * 2 * H], psum[:, 7, 0:T * 2 * H]))
                a_v, b_v = abv(lay)[:, :, 0:H], abv(lay)[:, :, H:2 * H]
                nc.vector.tensor_reduce(bmax_part[:, 0:H], b_v.rearrange("p t h -> p h t"), X, ALU.max)\
                    .then_inc(S[n, "bmax_part_made"], 1)
                nc.vector.tensor_copy(aht(lay).rearrange("p h t -> p t h"), a_v)\
                    .then_inc(S[n, "a_ht_made"], 1)
                thr_t = thrv(lay).rearrange("p h m t -> p m t h")
                nc.vector.tensor_scalar(thr_t[:, 0], b_v, BIG, TIE, ALU.mult, ALU.add)
                link(nc.vector.tensor_scalar(thr_t[:, 1], b_v, -1.0, None, ALU.mult))
                for s in range(2):
                    nc.vector.memset(vbuf(lay, s)[:, :, lay.DH:lay.C], 1.0)\
                        .then_inc(S[n, "exps_ready"], 1)
                dve.wait_ge(S[n, "bmax_made"], 1)
                tv = tmp[:, 0:T * H].rearrange("p (t h) -> p t h", t=T)
                tw = tmp2[:, 0:T * H].rearrange("p (t h) -> p t h", t=T)
                bm = bmax[:, 0:H].unsqueeze(1).broadcast_to([P, T, H])
                nc.vector.tensor_tensor(tv, b_v, bm, ALU.subtract)
                link(nc.vector.tensor_tensor(tw, a_v, bm, ALU.add))
                nc.vector.tensor_scalar(bb(lay)[:, :, :, 0], tv, 1.0, LIFT, ALU.mult, ALU.add)
                nc.vector.tensor_scalar(bb(lay)[:, :, :, 1], tv, 0.2, LIFT, ALU.mult, ALU.add)\
                    .then_inc(S[n, "exps_ready"], 1)
                w_t = wv(lay).rearrange("p h t m -> p m t h")
                nc.vector.tensor_scalar(w_t[:, 0], tw, 0.8, 0.0, ALU.mult, ALU.min)
                nc.vector.tensor_scalar(w_t[:, 1], tw, -0.8, 0.0, ALU.mult, ALU.min)\
                    .then_inc(S[n, "exps_ready"], 1)
                dve.wait_ge(S[n, "a_rows_ready"], 1)
                m = H * T // P
                nc.vector.tensor_copy(a_rows_sb[:, 0:m, :], psum[:, 6, 0:m * P].rearrange(
                    "p (c n) -> p c n", c=m)).then_inc(S[n, "a_rows_copied"], 1)

            def convert_adj(t):
                dve.wait_ge(adj_in_done[t % 2], 16 * (t // 2 + 1))
                nc.vector.tensor_scalar(adj8[:, t, :], adj_in[:, t % 2, :], 0.0, None, ALU.is_gt,
                                        saturate=False).then_inc(adj_made, 1)

            def prep(lay):
                n = lay.name

                def last_part(t):
                    dve.wait_ge(S[n, "mid_made"], t + 1)
                    dst = staged(lay, t // 2 % 2)
                    nc.vector.tensor_tensor(dst[:, :, t % 2, :, 2, :], xbuf(lay, t % 2),
                                            dst[:, :, t % 2, :, 1, :], ALU.subtract)\
                        .then_inc(S[n, "lo_made"], 1)

                dve.wait_ge(S[n, "exps_made"], 2)
                for t in range(T):
                    dve.wait_ge(S[n, "v_copied"], t + 1)
                    if t >= 2:
                        dve.wait_ge(S[n, "lo_made"], t - 1)
                    nc.vector.tensor_tensor(
                        xbuf(lay, t % 2),
                        vbuf(lay, t % 2).unsqueeze(2).broadcast_to([P, lay.H, 2, lay.C]),
                        bb(lay)[:, t, :, :].unsqueeze(3).broadcast_to([P, lay.H, 2, lay.C]),
                        ALU.mult).then_inc(S[n, "x_made"], 1)
                    if t >= 1:
                        last_part(t - 1)
                    dve.wait_ge(S[n, "hi_made"], t + 1)
                    nc.vector.tensor_tensor(xbuf(lay, t % 2), xbuf(lay, t % 2),
                                            staged(lay, t // 2 % 2)[:, :, t % 2, :, 0, :],
                                            ALU.subtract).then_inc(S[n, "r_made"], 1)
                    if lay is L0:
                        convert_adj(t)
                last_part(T - 1)

            def attention(lay):
                n = lay.name
                mine = lay.vector_tiles
                theirs = [t for t in range(T) if t not in mine]

                def thresholds(q, s):
                    nc.vector.tensor_copy(
                        thr_unit[:, s, :, :],
                        thrv(lay)[:, ds(head(lay, q, s), 1), :, :].rearrange("p o m t -> p (o m) t"))\
                        .then_inc(S[n, "thr_made"], 1)

                def mask(q, s, t, first):
                    slot = t % MASK_SLOTS
                    if t == MASK_SLOTS - 1:
                        if not first:
                            dve.wait_ge(S[n, "acc_ready"], 2 * BANKS * q + BANKS * s)
                    else:
                        done = t - (MASK_SLOTS - 1) if t >= MASK_SLOTS else t - (MASK_SLOTS - 2)
                        dve.wait_ge(S[n, "mask_slots_free"],
                                    2 * (T - 1) * q + ((T - 1) * s + done + MASK_SLOTS))
                    if t in mine:
                        c = mine.index(t)
                        dve.sem_inc(dve_gate, 1)
                        nc.vector.tensor_scalar(step_v[:, 0:lay.W], row(lay, s), thr_unit[:, s, 1, t:t + 1],
                                                None, ALU.is_ge, saturate=False)\
                            .then_inc(S[n, "compare_made"], 1)
                        dve.wait_ge(S[n, "compare_made"], 2 * len(mine) * q + (len(mine) * s + c + 1))
                        src = step_v[:, 0:lay.W]
                    else:
                        c = theirs.index(t)
                        dve.wait_ge(S[n, "step_made"], 2 * len(theirs) * q + (len(theirs) * s + c + 1))
                        src = steps[:, (c + s * len(theirs)) % STEP_SLOTS, 0:lay.W]
                    near = adj8[:, t, :] if lay.UH == 1 else adj8[:, t, s * lay.W:(s + 1) * lay.W]
                    nc.vector.tensor_tensor(masks(lay, slot, 0).bitcast(u32), src.bitcast(u32),
                                            near.bitcast(u32), ALU.bitwise_and)
                    nc.vector.scalar_tensor_tensor(
                        out=masks(lay, slot, 1).bitcast(u32), in0=src.bitcast(u32), scalar=ONES8,
                        in1=near.bitcast(u32), op0=ALU.bitwise_xor, op1=ALU.bitwise_and)\
                        .then_inc(S[n, "masks_made"], 1)

                c = PARTS * lay.C
                per = lay.per_bank * 2

                def drain_bank(q, s, b):
                    dve.wait_ge(S[n, "acc_ready"], 2 * BANKS * q + (BANKS * s + b + 1))
                    nc.vector.tensor_reduce(
                        num[:, s, b * per * lay.C:(b + 1) * per * lay.C].rearrange(
                            "p (g c) -> p g c", c=lay.C),
                        psum[:, b, 0:per * c].rearrange("p (g r c) -> p g c r", g=per, r=PARTS),
                        X, ALU.add).then_inc(S[n, "acc_free"], 1)

                def normalise(q, s, step):
                    size = lay.NI * lay.C
                    nv = num[:, s, 0:2 * size].rearrange("p (t m c) -> p t m c", t=lay.NI, m=2)
                    dn = den[:, 0:size].rearrange("p (t c) -> p t c", t=lay.NI)
                    rc = rec[:, 0:lay.NI]
                    if step == 0:
                        dve.wait_ge(S[n, "acc_free"], 2 * BANKS * q + (BANKS * s + 2 * BANKS))
                        w = wv(lay)[:, ds(head(lay, q, s), 1), cut(lay, q, s), :]\
                            .rearrange("p o t m -> p (o t) m")
                        nc.vector.tensor_tensor(nv, nv, w.unsqueeze(3).broadcast_to([P, lay.NI, 2, lay.C]),
                                                ALU.mult).then_inc(S[n, "norm_order"], 1)
                        return
                    dve.wait_ge(S[n, "norm_order"], 6 * q + (3 * s + step))
                    if step == 1:
                        nc.vector.tensor_tensor(dn, nv[:, :, 0, :], nv[:, :, 1, :], ALU.add)\
                            .then_inc(S[n, "norm_order"], 1)
                    elif step == 2:
                        nc.vector.reciprocal(rc, dn[:, :, lay.DH]).then_inc(S[n, "norm_order"], 1)
                    else:
                        nc.vector.tensor_tensor(
                            hid[:, cut(lay, q, s), ds(lay.DH * head(lay, q, s), lay.DH)],
                            dn[:, :, 0:lay.DH], rc.unsqueeze(2).broadcast_to([P, lay.NI, lay.DH]),
                            ALU.mult).then_inc(S[n, "hid_made"], 1)

                def rest(q, s, first):
                    for t in range(AHEAD, T):
                        mask(q, s, t, first)

                def lead(q, s, first=False):
                    thresholds(q, s)
                    dve.wait_ge(S[n, "thr_made"], 2 * q + (s + 1))
                    dve.wait_ge(S[n, f"row_loaded{s}"], 16 * q + 16)
                    for t in range(AHEAD):
                        mask(q, s, t, first)

                def unit_after(q, s, pq, ps_):
                    lead(q, s)
                    for b in range(BANKS):
                        drain_bank(pq, ps_, b)
                    for t in range(AHEAD, T):
                        mask(q, s, t, False)
                        if t - AHEAD < 4:
                            normalise(pq, ps_, t - AHEAD)

                dve.sem_inc(S[n, "masks_made"], T + STEP_SLOTS)
                dve.sem_inc(S[n, "acc_free"], BANKS)
                lead(0, 0, True)
                rest(0, 0, True)
                unit_after(0, 1, 0, 0)
                with dve.Fori(1, UNITS // 2, 1) as q:
                    unit_after(q, 0, q - 1, 1)
                    unit_after(q, 1, q, 0)
                last = UNITS // 2 - 1
                for b in range(BANKS):
                    drain_bank(last, 1, b)
                for step in range(4):
                    normalise(last, 1, step)

            scores_of_weights(L0, 0)
            factors(L0)
            prep(L0)
            for i in range(2):
                dve.wait_ge(S["l0", f"packs_out{i}"], 16 * (T // 4))
            attention(L0)

            dve.wait_ge(const_in, 160)

            def y_of(q, s):
                dve.wait_ge(o_ready, 2 * q + (s + 1))
                nc.vector.tensor_tensor(yb[:, s, :], psum[:, 2 + s, :], b_out_sb[:, :], ALU.add)\
                    .then_inc(y_made, 1)
                dve.wait_ge(y_made, 2 * q + (s + 1))
                nc.vector.tensor_scalar(eb[:, s, :], yb[:, s, :], 0.0, None, ALU.min).then_inc(m_made, 1)

            def stat(q, s, order):
                nc.vector.bn_stats(stats[:, s, :], resid[:, ds(2 * q + s, 1), :].rearrange("p o d -> p (o d)"))\
                    .then_inc(order, 1)
                dve.wait_ge(order, 8 * q + (4 * s + 3))
                dve.sem_inc(dve_gate, 1)
                nc.vector.bn_aggr(mv_tile[:, s, :], stats[:, s, :]).then_inc(order, 1)
                dve.wait_ge(order, 8 * q + (4 * s + 4))
                nc.vector.tensor_copy(mv[:, ds(2 * q + s, 1), :].rearrange("p o c -> p (o c)"), mv_tile[:, s, :])

            def z_of(q, s):
                tile = resid[:, ds(2 * q + s, 1), :].rearrange("p o d -> p (o d)")
                dve.wait_ge(e_made, 2 * q + (s + 1))
                nc.vector.scalar_tensor_tensor(out=eb[:, s, :], in0=eb[:, s, :], scalar=-1.0, in1=yb[:, s, :],
                                               op0=ALU.add, op1=ALU.max).then_inc(z_order, 1)
                dve.wait_ge(z_order, 8 * q + (4 * s + 1))
                dve.sem_inc(dve_gate, 1)
                dve.wait_ge(resid_in[s], 16 * q + 16)
                nc.vector.tensor_tensor(tile, eb[:, s, :], tile, ALU.add).then_inc(z_order, 1)
                dve.wait_ge(z_order, 8 * q + (4 * s + 2))
                dve.sem_inc(dve_gate, 1)
                stat(q, s, z_order)

            def inverse_std(made, back):
                link(nc.vector.drain())
                nc.vector.tensor_scalar(std[:, :], mv[:, :, 1], EPS, None, ALU.add).then_inc(made, 1)
                dve.wait_ge(back, 1)
                link(nc.vector.reciprocal(rstd[:, :], std[:, :]))

            def normed(q, s, made):
                tile = resid[:, ds(2 * q + s, 1), :].rearrange("p o d -> p (o d)")
                nc.vector.tensor_scalar(tile, tile,
                                        mv[:, ds(2 * q + s, 1), 0:1].rearrange("p o c -> p (o c)"),
                                        rstd[:, ds(2 * q + s, 1)], ALU.subtract, ALU.mult).then_inc(made, 1)

            y_of(0, 0)
            with dve.Fori(0, T // 2 - 1, 1) as q:
                y_of(q, 1)
                z_of(q, 0)
                y_of(q + 1, 0)
                z_of(q, 1)
            y_of(T // 2 - 1, 1)
            z_of(T // 2 - 1, 0)
            z_of(T // 2 - 1, 1)
            inverse_std(var_made, std_made)
            with dve.Fori(0, T // 2, 1) as q:
                for s in range(2):
                    normed(q, s, x1_made)

            scores_of_weights(L1, 1)
            factors(L1)
            prep(L1)
            for i in range(2):
                dve.wait_ge(S["l1", f"packs_out{i}"], 16 * (T // 4))
            attention(L1)

            def enc_of(t):
                if t >= 2:
                    dve.wait_ge(enc_made, t - 1)
                nc.vector.tensor_scalar(eb[:, t % 2, :], hid[:, t, :], 0.0, None, ALU.min)\
                    .then_inc(min_made, 1)

            def enc_end(t):
                dve.wait_ge(exp_made, t + 1)
                nc.vector.scalar_tensor_tensor(out=hid[:, t, :], in0=eb[:, t % 2, :], scalar=-1.0,
                                               in1=hid[:, t, :], op0=ALU.add, op1=ALU.max)\
                    .then_inc(enc_made, 1)

            def final(t):
                q, s = t // 2, t % 2
                tile = resid[:, t, :]
                dve.wait_ge(f_ready, t + 1)
                nc.vector.tensor_tensor(yb[:, s, :], psum[:, 7 if s else 4, :], b4_sb[:, :], ALU.add)\
                    .then_inc(f_read, 1)
                dve.wait_ge(f_read, t + 1)
                dve.wait_ge(x1_back[t % 2], 16 * (t // 2 + 1))
                nc.vector.tensor_tensor(tile, yb[:, s, :], tile, ALU.add).then_inc(g_order, 1)
                dve.wait_ge(g_order, 2 * t + 1)
                nc.vector.bn_stats(stats[:, s, :], tile).then_inc(g_order, 1)
                dve.wait_ge(g_order, 2 * t + 2)
                nc.vector.bn_aggr(mv[:, t, :], stats[:, s, :])

            dve.wait_ge(S["l1", "hid_made"], UNITS)
            for c in range(5):
                if c < 4:
                    for t in range(4 * c, 4 * c + 4):
                        enc_of(t)
                        if t > 4 * c:
                            enc_end(t - 1)
                    enc_end(4 * c + 3)
                if c >= 1:
                    for t in range(4 * c - 4, 4 * c):
                        final(t)
            inverse_std(var2_made, std2_made)
            with dve.Fori(0, T // 2, 1) as q:
                for s in range(2):
                    normed(q, s, out_made)

        @block.tensor
        def _(pe):
            def project(lay):
                n, H = lay.name, lay.H
                if lay is L0:
                    pe.wait_ge(x_in, 16 * KT)
                else:
                    pe.wait_ge(x1T_copied, T)
                pe.wait_ge(S[n, "wa_made"], 1)
                for t in range(T):
                    for k in range(KT):
                        last = nc.tensor.matmul(psum[:, 7, t * 2 * H:(t + 1) * 2 * H],
                                                featT[:, k, t * P:(t + 1) * P], wa[:, k, 0:2 * H],
                                                start=(k == 0), stop=(k == KT - 1))
                last.then_inc(S[n, "ab_ready"], 1)

                def v_of(t):
                    if t >= VOUT:
                        pe.wait_ge(S[n, "v_copied"], t - VOUT + 1)
                    for k in range(KT):
                        last = nc.tensor.matmul(psum[:, t % VOUT, :], featT[:, k, t * P:(t + 1) * P],
                                                w_proj[:, k, :], start=(k == 0), stop=(k == KT - 1))
                    last.then_inc(S[n, "v_ready"], 1)

                for t in range(VOUT):
                    v_of(t)
                pe.wait_ge(S[n, "a_ht_made"], 1)
                pe.wait_ge(ident_step, 2)
                for c in range(H * T // P):
                    last = nc.tensor.transpose(psum[:, 6, c * P:(c + 1) * P], a_ht[:, c * P:(c + 1) * P],
                                               ident[:, :])
                last.then_inc(S[n, "a_rows_ready"], 1)
                for t in range(VOUT, T):
                    v_of(t)

            def attention(lay):
                n = lay.name
                pe.wait_ge(S[n, "v_copied"], T)
                pe.wait_ge(S[n, "a_rows_copied"], 1)
                pe.sem_inc(S[n, "mask_slots_free"], MASK_SLOTS)
                with pe.Fori(0, UNITS // 2, 1) as q:
                    for s in range(2):
                        pe.wait_ge(S[n, f"pack_loaded{s}"], 16 * q + 16)
                        pe.sem_inc(pe_gate, 1)
                        for t in range(T):
                            pe.wait_ge(S[n, "masks_made"],
                                       32 * q + (T * s + t + 1 + T + STEP_SLOTS))
                            pe.sem_inc(pe_gate, 1)
                            for it in range(lay.NI):
                                b, first = it // lay.per_bank, it % lay.per_bank == 0
                                if t == 0 and first:
                                    pe.wait_ge(S[n, "acc_free"], 2 * BANKS * q + (BANKS * s + b + 1))
                                    pe.sem_inc(pe_gate, 1)
                                for m in range(2):
                                    last = nc.tensor.matmul(
                                        bank_out(lay, it, m),
                                        masks(lay, t % MASK_SLOTS, m)[:, it * P:(it + 1) * P],
                                        pack(lay, s)[:, t, m, :],
                                        start=(t == 0 and first and m == 0), stop=(t == T - 1),
                                        skip_group_check=True)
                                if t == T - 1 and it % lay.per_bank == lay.per_bank - 1:
                                    last.then_inc(S[n, "acc_ready"], 1)
                            if t < T - 1:
                                last.then_inc(S[n, "mask_slots_free"], 1)

            project(L0)
            attention(L0)

            pe.wait_ge(S["l0", "hid_made"], UNITS)
            pe.wait_ge(S["l0", "acc_free"], BANKS * UNITS + BANKS)
            pe.wait_ge(const_in, 160)

            def transposes(t, bank):
                for k in range(KT):
                    last = nc.tensor.transpose(psum[:, bank, k * P:(k + 1) * P],
                                               hid[:, t, k * P:(k + 1) * P], ident[:, :])
                return last

            transposes(0, 0).then_inc(t_ready, 1)
            for t in range(T):
                if t + 1 < T:
                    if t >= 1:
                        pe.wait_ge(t_copied, t)
                    transposes(t + 1, (t + 1) % 2).then_inc(t_ready, 1)
                pe.wait_ge(t_copied, t + 1)
                if t >= 2:
                    pe.wait_ge(y_made, t - 1)
                for k in range(KT):
                    last = nc.tensor.matmul(psum[:, 2 + t % 2, :], hT[:, t % 2, k, :], w_out_sb[:, k, :],
                                            start=(k == 0), stop=(k == KT - 1))
                last.then_inc(o_ready, 1)
            for t in range(T):
                pe.wait_ge(x1_made, t + 1)
                if t >= 2:
                    pe.wait_ge(x1T_copied, t - 1)
                for k in range(KT):
                    last = nc.tensor.transpose(psum[:, 4 + t % 2, k * P:(k + 1) * P],
                                               resid[:, t, k * P:(k + 1) * P], ident[:, :])
                last.then_inc(x1T_ready, 1)

            project(L1)
            attention(L1)

            pe.wait_ge(S["l1", "acc_free"], BANKS * UNITS + BANKS)
            def turn_chunk(c):
                for t in range(4 * c, 4 * c + 4):
                    pe.wait_ge(enc_made, t + 1)
                    if t >= 2:
                        pe.wait_ge(e_copied, t - 1)
                    transposes(t, t % 2).then_inc(e_ready, 1)

            turn_chunk(0)
            for c in range(4):
                if c < 3:
                    turn_chunk(c + 1)
                pe.wait_ge(e_copied, 4 * c + 4)
                for f in range(2):
                    if c >= 1:
                        pe.wait_ge(h_made, 5 * c - 5 + f + 1)
                    for k in range(KT):
                        last = nc.tensor.matmul(psum[:, 2 + f, :], w1_sb[:, k, f * P:(f + 1) * P],
                                                encT[:, c % 2, k, :], start=(k == 0), stop=(k == KT - 1))
                    last.then_inc(h_ready, 1)
                pe.wait_ge(h_made, 5 * c + 2)
                if c >= 1:
                    pe.wait_ge(f_read, 4 * c)
                for k in range(2):
                    last = nc.tensor.matmul(psum[:, 4, :], w2_sb[:, k, :], h1T[:, k, :],
                                            start=(k == 0), stop=(k == 1))
                last.then_inc(h_ready, 1)
                pe.wait_ge(h_made, 5 * c + 3)
                for f in range(2):
                    nc.tensor.matmul(psum[:, 5 + f, :], w3_sb[:, f * P:(f + 1) * P], h2T,
                                     start=True, stop=True).then_inc(h_ready, 1)
                pe.wait_ge(h_made, 5 * c + 5)
                for t in range(4 * c, 4 * c + 4):
                    if t >= 2:
                        pe.wait_ge(f_read, t - 1)
                    for k in range(2):
                        last = nc.tensor.matmul(psum[:, 7 if t % 2 else 4, :],
                                                h3T[:, k, t % 4 * P:(t % 4 + 1) * P], w4_sb[:, k, :],
                                                start=(k == 0), stop=(k == 1))
                    last.then_inc(f_ready, 1)


def kernel(x, adj, L0_gnn_W_seq, L0_gnn_a1, L0_gnn_a2, L0_gnn_W_out, L0_gnn_b_out, L1_gnn_W, L1_gnn_a1,
           L1_gnn_a2, L1_gnn_W1, L1_gnn_b1, L1_gnn_W2, L1_gnn_b2, L1_gnn_W3, L1_gnn_b3, L1_gnn_W4, L1_gnn_b4):
    import numpy as np
    import concourse.bacc as bacc
    from concourse import mybir as mb
    from concourse.bass_utils import run_bass_kernel_spmd

    def flat(a, *shape):
        return np.ascontiguousarray(np.asarray(a)).reshape(*shape)

    def turned(a):
        return np.ascontiguousarray(np.asarray(a).T)

    def columns(a, n):
        return np.ascontiguousarray(np.asarray(a).reshape(n, 128).T)

    nc = bacc.Bacc("TRN2", target_bir_lowering=False, num_devices=1)
    arrays = {
        "xT": turned(x), "x": flat(x, N, D), "adjT": turned(adj),
        "w_seq": flat(L0_gnn_W_seq, D, D), "a1_0": flat(L0_gnn_a1, 1, -1), "a2_0": flat(L0_gnn_a2, 1, -1),
        "w_out": flat(L0_gnn_W_out, D, D), "b_out": flat(L0_gnn_b_out, 1, D),
        "w_heads": np.ascontiguousarray(np.asarray(L1_gnn_W).transpose(1, 0, 2)).reshape(D, D),
        "a1_1": flat(L1_gnn_a1, 1, D), "a2_1": flat(L1_gnn_a2, 1, D),
        "w1T": turned(L1_gnn_W1), "b1": columns(L1_gnn_b1, 2),
        "w2T": turned(L1_gnn_W2), "b2": columns(L1_gnn_b2, 1),
        "w3T": turned(L1_gnn_W3), "b3": columns(L1_gnn_b3, 2),
        "w4T": turned(L1_gnn_W4), "b4": flat(L1_gnn_b4, 1, D),
    }
    args = [nc.dram_tensor(n, a.shape, mb.dt.from_np(a.dtype), kind="ExternalInput").ap()
            for n, a in arrays.items()]
    out = nc.dram_tensor("out", (T, P, D), mb.dt.float32, kind="ExternalOutput").ap()
    packs = nc.dram_tensor("packs", (16 * P * T * 2 * PARTS * 33,), mb.dt.bfloat16).ap()
    rows = nc.dram_tensor("rows", (16, N), mb.dt.float32).ap()
    x1_keep = nc.dram_tensor("x1_keep", (T, P, D), mb.dt.float32).ap()
    gat_kernel(nc, *args, out, packs, rows, x1_keep)
    r = run_bass_kernel_spmd(nc, [arrays], core_ids=[0])
    return r.results[0]["out"].reshape(N, D)
```

```python
from contextlib import ExitStack

import concourse.bass as bass
from concourse import mybir

ds = bass.ds

P = 128
N = 2048
D = 512
T = N // P
KT = D // P
PARTS = 3
UNITS = 16
MASK_SLOTS = 8
STEP_SLOTS = 6
AHEAD = 3
NORM_AT = (6, 8, 10, 12)
THR_AT, HIGH_AT, MIDDLE_AT, BUILD_AT = 9, 10, 13, (4, 11, 15)
BANKS = 8
ADJ_SLOTS = 4
MASKS0 = 2 * T
BIG = 2.0 ** 80
TIE = 60.0
MINUS8 = 0xB8B8B8B8
LIFT = 64.0
EPS = 1e-5


def slot_rounds(count, slots):
    rounds = -(-count // slots)
    slot = [i for r in range(rounds) for i in range(count // rounds + (r < count % rounds))]
    last = [max(j for j in range(i - count, i) if slot[j % count] == slot[i]) for i in range(count)]
    return slot, last


class Layer:

    def __init__(self, name, heads, body_units, vector_tiles, whole_tiles):
        self.name = name
        self.H = heads
        self.DH = D // heads
        self.C = self.DH + 1
        self.W = heads * N // UNITS
        self.NI = self.W // P
        self.per_bank = self.NI // BANKS
        self.UH = UNITS // heads
        self.PT = T // self.UH
        self.TILE = 2 * PARTS * self.C
        self.SB = body_units
        self.Q = UNITS // body_units
        self.vector_tiles = vector_tiles
        self.whole_tiles = whole_tiles
        self.scalar_tiles = [t for t in range(T) if t not in vector_tiles]
        self.step_slot, self.step_last = slot_rounds(len(self.scalar_tiles) * body_units, STEP_SLOTS)

    def head(self, q, s):
        return self.SB // self.UH * q + s // self.UH

    def pack_slot(self, s):
        return s // self.UH % 2

    def half(self, s):
        return s % self.UH


L0 = Layer("l0", 16, 2, (4, 9, 14), (0, 2, 4, 5, 6, 8, 10, 12, 14))
L1 = Layer("l1", 8, 4, (), ())
LAYERS = (L0, L1)


def gat_kernel(nc, xT, x, adjT, w_seq, a1_0, a2_0, w_out, b_out, w_heads, a1_1, a2_1,
               w1T, b1, w2T, b2, w3T, b3, w4T, b4, out, rows, x1_keep):
    dt = mybir.dt
    ALU = mybir.AluOpType
    ACT = mybir.ActivationFunctionType
    X = mybir.AxisListType.X
    f32, bf16, f8, u32 = dt.float32, dt.bfloat16, dt.float8e4, dt.uint32
    RMAX = bass.bass_isa.ReduceOp.max

    ctx = ExitStack()
    with ctx:
        def sb(name, shape, dtype):
            return ctx.enter_context(nc.sbuf_tensor(name, shape, dtype))

        def sem(name):
            return ctx.enter_context(nc.semaphore(name))

        near8 = sb("near8", [P, T, N], f8)
        feat = sb("feat", [P, T, D], f32)
        featT = feat[:, :, :].rearrange("p t (k n) -> p t k n", k=KT)
        vals = sb("vals", [P, T, D], f32)
        w_proj = sb("w_proj", [P, 2, KT, D], f32)
        net_w = w_proj[:, :, :, :].rearrange("p i k n -> p (i k n)")
        w1_sb = net_w[:, 0:1024].rearrange("p (k n) -> p k n", k=KT)
        w4_sb = net_w[:, 1024:2048].rearrange("p (k n) -> p k n", k=2)
        w2_sb = net_w[:, 2048:2304].rearrange("p (k n) -> p k n", k=2)
        w3_sb = net_w[:, 2304:2560]
        b4_sb = net_w[:, 2560:3072]
        b_out_sb = sb("b_out_sb", [P, D], f32)
        b1_sb = sb("b1_sb", [P, 2], f32)
        b2_sb = sb("b2_sb", [P, 1], f32)
        b3_sb = sb("b3_sb", [P, 2], f32)
        ident = sb("ident", [P, P], f32)
        wa = sb("wa", [P, 2, KT, 32], f32)
        steps = sb("steps", [P, STEP_SLOTS, N], f8)
        before_steps = steps[:, STEP_SLOTS - 2:, :].rearrange("p s n -> p (s n)").bitcast(f32)
        ab = before_steps[:, 0:T * 32]
        tmp = before_steps[:, T * 32:T * 48]
        tmp2 = before_steps[:, T * 48:T * 64]
        bmax_part = sb("bmax_part", [P, 16], f32)
        bmax = sb("bmax", [P, 16], f32)
        BB = sb("BB", [P, T * 16 * 2], f32)
        ww = sb("ww", [P, T * 16 * 2], f32)
        thr = sb("thr", [P, T * 16 * 2], f32)
        thr_unit = sb("thr_unit", [P, 2, 2, T], f32)
        prod = sb("prod", [P, 1056], f32)
        step_v = sb("step_v", [P, N], f8)
        num = sb("num", [P, 1056], f32)
        den = sb("den", [P, 528], f32)
        rec = sb("rec", [P, T], f32)
        stats = sb("stats", [P, 2, 6], f32)
        mv = sb("mv", [P, T, 2], f32)
        std = sb("std", [P, T], f32)
        rstd = sb("rstd", [P, T], f32)

        RING0, ROW0 = 0, MASK_SLOTS * 2 * L0.W
        PACK0 = ROW0 + 2 * 4 * L0.W
        RING1, ROW1 = 0, MASK_SLOTS * 2 * L1.W
        PACK1 = ROW1 + 2 * 4 * L1.W
        ARENA = PACK0 + 2 * 2 * T * L0.TILE
        ROW_AT = {"l0": ROW0, "l1": ROW1}
        PACK_AT = {"l0": PACK0, "l1": PACK1}
        arena = sb("arena", [P, ARENA // 4], f32)
        flat = arena[:, :]
        adj_in = flat[:, 0:ADJ_SLOTS * N].rearrange("p (s n) -> p s n", s=ADJ_SLOTS)
        wprod = flat[:, ROW0 // 4:ROW0 // 4 + N]
        a_bc = flat[:, ROW0 // 4 + N:ROW0 // 4 + 2 * N].rearrange("p (v n) -> p v n", v=4)
        resid = flat[:, 0:T * D].rearrange("p (t d) -> p t d", t=T)
        scT = flat[0:32, 13312:13312 + N]
        TMP = T * D
        yb = flat[:, TMP:TMP + 2 * D].rearrange("p (s d) -> p s d", s=2)
        eb = flat[:, TMP + 2 * D:TMP + 4 * D].rearrange("p (s d) -> p s d", s=2)
        hT = flat[:, TMP + 4 * D:TMP + 6 * D].rearrange("p (s k n) -> p s k n", s=2, k=KT)
        h1T = flat[:, TMP + 4 * D:TMP + 6 * D].rearrange("p (f n) -> p f n", f=2)
        h2T = flat[:, TMP + 6 * D:TMP + 7 * D]
        h3T = flat[:, TMP + 7 * D:TMP + 9 * D].rearrange("p (f n) -> p f n", f=2)
        encT = vals[:, 0:8, :].rearrange("p (s k) n -> p s k n", s=2)

        psum = ctx.enter_context(nc.psum_tensor("psum", [P, BANKS, 512], f32))

        x_in = [sem(f"x_in_{c}") for c in range(4)]
        w_in = [sem(f"w_in_{i}") for i in range(3)]
        a_in = [sem(f"a_in_{i}") for i in range(2)]
        const_in = sem("const_in")
        net_in = sem("net_in")
        adj_in_done = [sem(f"adj_in_done_{i}") for i in range(ADJ_SLOTS)]
        adj_made = sem("adj_made")
        ident_step = sem("ident_step")
        dve_order = sem("dve_order")
        pe_gate = sem("pe_gate")
        act_gate = sem("act_gate")
        dve_gate = sem("dve_gate")
        S = {}
        for lay in LAYERS:
            for what in ("wa_made", "scores_ready", "scores_copied", "ab_ready", "bmax_part_made",
                         "bmax_made", "exps_ready", "exps_made", "a_rows_out",
                         "v_ready", "v_copied", "x_made", "hi_made", "r_made", "mid_made", "lo_made",
                         "row_loaded0", "row_loaded1", "thr_made", "step_made",
                         "compare_made", "masks_made", "mask_slots_free", "acc_ready", "acc_free",
                         "norm_order", "hid_made"):
                S[lay.name, what] = sem(f"{lay.name}_{what}")
        resid_in = [sem(f"resid_in_{i}") for i in range(2)]
        h_turned = sem("h_turned")
        h_copied = sem("h_copied")
        o_ready = sem("o_ready")
        y_made = sem("y_made")
        m_made = sem("m_made")
        e_made = sem("e_made")
        z_order = sem("z_order")
        var_made = sem("var_made")
        std_made = sem("std_made")
        x1_made = sem("x1_made")
        x1_turned = sem("x1_turned")
        x1_copied = sem("x1_copied")
        x1_out = sem("x1_out")
        x1_back = [sem(f"x1_back_{i}") for i in range(2)]
        min_made = sem("min_made")
        exp_made = sem("exp_made")
        enc_made = sem("enc_made")
        e_turned = sem("e_turned")
        e_copied = sem("e_copied")
        h_ready = sem("h_ready")
        h_made = sem("h_made")
        f_ready = sem("f_ready")
        f_read = sem("f_read")
        g_order = sem("g_order")
        var2_made = sem("var2_made")
        std2_made = sem("std2_made")
        out_made = sem("out_made")
        out_done = sem("out_done")

        def bb(lay):
            return BB[:, 0:T * lay.H * 2].rearrange("p (t h m) -> p t h m", t=T, m=2)

        def wv(lay):
            return ww[:, 0:T * lay.H * 2].rearrange("p (h t m) -> p h t m", t=T, m=2)

        def thrv(lay):
            return thr[:, 0:T * lay.H * 2].rearrange("p (h m t) -> p h m t", t=T, m=2)

        def abv(lay):
            return ab[:, 0:T * 2 * lay.H].rearrange("p (t c) -> p t c", t=T)

        def prodv(lay):
            return prod[:, 0:lay.PT * 2 * lay.C].rearrange("p (t m c) -> p t m c", t=lay.PT, m=2)

        def masks(lay, slot, m):
            o = (slot * 2 + m) * lay.W
            return flat.bitcast(f8)[:, o:o + lay.W]

        def row(lay, slot):
            o = ROW_AT[lay.name] // 4 + slot * lay.W
            return flat[:, o:o + lay.W]

        def pack(lay, slot):
            o = PACK_AT[lay.name] // 2 + slot * T * lay.TILE
            return flat.bitcast(bf16)[:, o:o + T * lay.TILE].rearrange(
                "p (t m r c) -> p t m r c", t=T, m=2, r=PARTS)

        def bank_out(lay, it, m0, m1):
            c = PARTS * lay.C
            o = (it % lay.per_bank) * 2 * c
            return psum[:, it // lay.per_bank, o + m0 * c:o + m1 * c]

        def near(lay, s, t):
            return near8[:, t, lay.half(s) * lay.W:(lay.half(s) + 1) * lay.W]

        def v_bank(lay, t):
            return 4 + t % 3 if lay is L0 else 6 if t < 12 else 4 + t % 2

        BLOCK = 3
        FREED = T - BLOCK

        block = ctx.enter_context(nc.Block())

        @block.sync
        def _(sp):
            def store_rows(lay):
                sp.wait_ge(S[lay.name, "scores_copied"], 4)
                sp.dma_start(rows[0:lay.H, :], scT[0:lay.H, :]).then_inc(S[lay.name, "a_rows_out"], 16)

            def load_row(lay, q, s):
                units = rows[0:lay.H, :].rearrange("h (g n) -> (h g) n", g=lay.UH)
                sp.dma_start(row(lay, s), units[ds(2 * q + s, 1), :].partition_broadcast(P))\
                    .then_inc(S[lay.name, f"row_loaded{s}"], 16)

            def first_rows(lay):
                sp.wait_ge(S[lay.name, "a_rows_out"], 16)
                for s in range(2):
                    load_row(lay, 0, s)

            def later_rows(lay):
                with sp.Fori(1, UNITS // 2, 1) as q:
                    for s in range(2):
                        sp.wait_ge(S[lay.name, "masks_made"], 2 * T * q + (T * s - T + MASKS0))
                        load_row(lay, q, s)

            sp.dma_start(w_proj[:, 0, :, :], w_seq.rearrange("(k p) n -> p k n", p=P)).then_inc(w_in[0], 16)
            for v, src in enumerate((a1_0, a2_0)):
                sp.dma_start(a_bc[:, v, 0:L0.DH], src.partition_broadcast(P)).then_inc(a_in[0], 16)
            for c in range(4):
                sp.dma_start(featT[:, 4 * c:4 * c + 4, :, :].rearrange("p t k n -> p (t k n)"),
                             xT[:, c, :]).then_inc(x_in[c], 16)
            for t in range(T):
                if t >= ADJ_SLOTS:
                    sp.wait_ge(adj_made, t - ADJ_SLOTS + 1)
                sp.dma_start(adj_in[:, t % ADJ_SLOTS, :], adjT[t * P:(t + 1) * P, :])\
                    .then_inc(adj_in_done[t % ADJ_SLOTS], 16)
                if t == 5:
                    sp.dma_start(w_proj[:, 1, :, :], w_heads.rearrange("(k p) n -> p k n", p=P))\
                        .then_inc(w_in[1], 16)
                    for v, src in enumerate((a1_1, a2_1)):
                        sp.dma_start(a_bc[:, 2 + v, :], src.partition_broadcast(P)).then_inc(a_in[1], 16)
                if t == 7:
                    store_rows(L0)
            sp.wait_ge(S["l1", "wa_made"], 1)
            first_rows(L0)
            for dst, src in ((b_out_sb[:, :], b_out.partition_broadcast(P)),
                             (b1_sb[:, :], b1), (b2_sb[:, :], b2), (b3_sb[:, :], b3)):
                sp.dma_start(dst, src).then_inc(const_in, 16)
            sp.wait_ge(S["l0", "v_ready"], T)
            sp.dma_start(w_proj[:, 0, :, :], w_out.rearrange("(k p) n -> p k n", p=P)).then_inc(w_in[2], 16)
            later_rows(L0)

            sp.wait_ge(S["l0", "acc_ready"], BANKS * UNITS)
            for t in range(T):
                if t >= 2:
                    sp.wait_ge(resid_in[t % 2], 16 * (t // 2))
                sp.dma_start(resid[:, t, :], x[t * P:(t + 1) * P, :]).then_inc(resid_in[t % 2], 16)
            with sp.Fori(0, T // 2, 1) as q:
                for s in range(2):
                    sp.wait_ge(x1_made, 2 * q + (s + 1))
                    sp.dma_start(x1_keep[ds(2 * q + s, 1), :, :].rearrange("o p d -> p (o d)"),
                                 resid[:, ds(2 * q + s, 1), :].rearrange("p o d -> p (o d)"))\
                        .then_inc(x1_out, 16)
            store_rows(L1)
            sp.wait_ge(x1_out, 16 * T)
            sp.wait_ge(x1_turned, T)
            first_rows(L1)
            sp.wait_ge(S["l1", "v_ready"], T)
            for dst, src in ((w1_sb, w1T.rearrange("(k p) n -> p k n", p=P)),
                             (w2_sb, w2T.rearrange("(k p) n -> p k n", p=P)),
                             (w3_sb, w3T),
                             (w4_sb, w4T.rearrange("(k p) n -> p k n", p=P)),
                             (b4_sb, b4.partition_broadcast(P))):
                sp.dma_start(dst, src).then_inc(net_in, 16)
            later_rows(L1)

            sp.wait_ge(S["l1", "acc_ready"], BANKS * UNITS)
            for t in range(T):
                if t >= 2:
                    sp.wait_ge(x1_back[t % 2], 16 * (t // 2))
                sp.dma_start(resid[:, t, :], x1_keep[t, :, :]).then_inc(x1_back[t % 2], 16)
            with sp.Fori(0, T // 2, 1) as q:
                for s in range(2):
                    sp.wait_ge(out_made, 2 * q + (s + 1))
                    sp.dma_start(out[ds(2 * q + s, 1), :, :].rearrange("o p d -> p (o d)"),
                                 resid[:, ds(2 * q + s, 1), :].rearrange("p o d -> p (o d)"))\
                        .then_inc(out_done, 16)
            sp.wait_ge(out_done, 16 * T)

        @block.gpsimd
        def _(pool):
            nc.gpsimd.memset(ident[:, :], 0.0).then_inc(ident_step, 1)
            pool.wait_ge(ident_step, 1)
            nc.gpsimd.affine_select(out=ident[:, :], in_=ident[:, :], compare_op=ALU.not_equal, fill=1.0,
                                    base=0, pattern=[[-1, P]], channel_multiplier=1)\
                .then_inc(ident_step, 1)
            for lay in LAYERS:
                pool.wait_ge(S[lay.name, "bmax_part_made"], 1)
                nc.gpsimd.partition_all_reduce(bmax[:, 0:lay.H], bmax_part[:, 0:lay.H], P, RMAX)\
                    .then_inc(S[lay.name, "bmax_made"], 1)

        @block.scalar
        def _(act):
            def exps(lay):
                n = lay.name
                act.wait_ge(S[n, "exps_ready"], 2)
                nc.scalar.activation(BB[:, 0:T * lay.H * 2], BB[:, 0:T * lay.H * 2], ACT.Exp)\
                    .then_inc(S[n, "exps_made"], 1)
                nc.scalar.activation(ww[:, 0:T * lay.H * 2], ww[:, 0:T * lay.H * 2], ACT.Exp)\
                    .then_inc(S[n, "exps_made"], 1)

            def copy_v(lay, t):
                act.wait_ge(S[lay.name, "v_ready"], t + 1)
                nc.scalar.activation(vals[:, t, :], psum[:, v_bank(lay, t), :], ACT.Copy)\
                    .then_inc(S[lay.name, "v_copied"], 1)

            def part_of(lay, slot, g):
                return pack(lay, slot)[:, g * lay.PT:(g + 1) * lay.PT]

            def high(lay, slot, g, n_made):
                act.wait_ge(S[lay.name, "x_made"], n_made)
                nc.scalar.activation(part_of(lay, slot, g)[:, :, :, 0, :], prodv(lay), ACT.Copy)\
                    .then_inc(S[lay.name, "hi_made"], 1)

            def middle(lay, slot, g, n_made):
                act.wait_ge(S[lay.name, "r_made"], n_made)
                nc.scalar.activation(part_of(lay, slot, g)[:, :, :, 1, :], prodv(lay), ACT.Copy)\
                    .then_inc(S[lay.name, "mid_made"], 1)

            def compares(lay):
                n = lay.name
                mine = lay.scalar_tiles
                for g in range(lay.UH):
                    high(lay, 0, g, g + 1)
                    middle(lay, 0, g, g + 1)

                def unit(q, s, build):
                    act.wait_ge(S[n, f"row_loaded{s % 2}"], 16 * (lay.SB // 2) * q + 16 * (s // 2 + 1))
                    act.wait_ge(S[n, "thr_made"], lay.SB * q + (s + 1))
                    for c, t in enumerate(mine):
                        use = c + s * len(mine)
                        last = lay.step_last[use]
                        last_tile = last // len(mine) * T + mine[last % len(mine)]
                        act.wait_ge(S[n, "masks_made"],
                                    T * lay.SB * q + (last_tile + 1 + MASKS0))
                        act.sem_inc(act_gate, 1)
                        nc.scalar.activation(steps[:, lay.step_slot[use], 0:lay.W],
                                             row(lay, s % 2), ACT.Sigmoid,
                                             bias=thr_unit[:, s % 2, 0, t:t + 1], scale=BIG, saturate=False)\
                            .then_inc(S[n, "step_made"], 1)
                        nxt = s + lay.UH
                        if build and t == HIGH_AT:
                            if lay.half(s) == 0 and not (isinstance(q, int) and q == 0 and s == 0):
                                act.wait_ge(S[n, "acc_ready"], BANKS * lay.SB * q + BANKS * s)
                            high(lay, lay.pack_slot(nxt), lay.half(s), lay.SB * q + (s + 1 + lay.UH))
                        if build and t == MIDDLE_AT:
                            middle(lay, lay.pack_slot(nxt), lay.half(s), lay.SB * q + (s + 1 + lay.UH))

                for s in range(lay.SB):
                    unit(0, s, True)
                with act.Fori(1, lay.Q - 1, 1) as q:
                    for s in range(lay.SB):
                        unit(q, s, True)
                for s in range(lay.SB):
                    unit(lay.Q - 1, s, s < lay.SB - lay.UH)

            for t in range(8):
                copy_v(L0, t)
            exps(L0)
            for t in range(8, T):
                copy_v(L0, t)
            act.wait_ge(S["l0", "a_rows_out"], 16)
            compares(L0)

            for t in range(-1, T + 6):
                if 0 <= t + 1 < T:
                    act.wait_ge(h_turned, t + 2)
                    nc.scalar.activation(hT[:, (t + 1) % 2, :, :],
                                         psum[:, (t + 1) % 2, :].rearrange("p (k n) -> p k n", k=KT),
                                         ACT.Copy).then_inc(h_copied, 1)
                if t >= 4 and t % 4 == 0 and t <= T:
                    g = t // 4 - 1
                    act.wait_ge(var_made, g + 1)
                    nc.scalar.activation(std[:, 4 * g:4 * g + 4], std[:, 4 * g:4 * g + 4], ACT.Sqrt)\
                        .then_inc(std_made, 1)
                if 0 <= t < T:
                    act.wait_ge(m_made, t + 1)
                    nc.scalar.activation(eb[:, t % 2, :], eb[:, t % 2, :], ACT.Exp).then_inc(e_made, 1)
                if 0 <= t - 6 < T:
                    act.wait_ge(x1_turned, t - 5)
                    nc.scalar.activation(feat[:, t - 6, :], psum[:, 4 + (t - 6) % 2, :], ACT.Copy)\
                        .then_inc(x1_copied, 1)
                if 0 <= t - 7 < 12:
                    copy_v(L1, t - 7)
            for t in range(12, 15):
                copy_v(L1, t)
            exps(L1)
            copy_v(L1, 15)
            act.wait_ge(S["l1", "a_rows_out"], 16)
            act.wait_ge(x1_out, 16 * T)
            compares(L1)

            def enc_exp(t):
                act.wait_ge(min_made, t + 1)
                nc.scalar.activation(eb[:, t % 2, :], eb[:, t % 2, :], ACT.Exp).then_inc(exp_made, 1)

            def enc_copy(t):
                act.wait_ge(e_turned, t + 1)
                nc.scalar.activation(encT[:, t // 4 % 2, :, t % 4 * P:(t % 4 + 1) * P],
                                     psum[:, t % 2, :].rearrange("p (k n) -> p k n", k=KT),
                                     ACT.Copy).then_inc(e_copied, 1)

            def relu(c, i, dst, bank, bias):
                act.wait_ge(h_ready, 5 * c + i + 1)
                nc.scalar.activation(dst, psum[:, bank, :], ACT.Relu, bias=bias).then_inc(h_made, 1)

            for t in range(4):
                enc_exp(t)
                if t:
                    enc_copy(t - 1)
            enc_copy(3)
            for c in range(4):
                more = c < 3
                n = 4 * c + 4
                relu(c, 0, h1T[:, 0, :], 2, b1_sb[:, 0:1])
                if more:
                    enc_exp(n)
                relu(c, 1, h1T[:, 1, :], 3, b1_sb[:, 1:2])
                if more:
                    enc_exp(n + 1)
                relu(c, 2, h2T, 4, b2_sb[:, 0:1])
                if more:
                    enc_copy(n)
                    enc_exp(n + 2)
                    enc_copy(n + 1)
                    enc_exp(n + 3)
                    enc_copy(n + 2)
                    enc_copy(n + 3)
                relu(c, 3, h3T[:, 0, :], 5, b3_sb[:, 0:1])
                relu(c, 4, h3T[:, 1, :], 4, b3_sb[:, 1:2])
                if c >= 1:
                    act.wait_ge(var2_made, c)
                    nc.scalar.activation(std[:, 4 * c - 4:4 * c], std[:, 4 * c - 4:4 * c], ACT.Sqrt)\
                        .then_inc(std2_made, 1)
            act.wait_ge(var2_made, 4)
            nc.scalar.activation(std[:, 12:16], std[:, 12:16], ACT.Sqrt).then_inc(std2_made, 1)

        @block.vector
        def _(dve):
            ordered = [0]

            def link(ins):
                ordered[0] += 1
                ins.then_inc(dve_order, 1)
                dve.wait_ge(dve_order, ordered[0])

            def scores_of_weights(lay, i):
                dve.wait_ge(w_in[i], 16)
                dve.wait_ge(a_in[i], 32)
                length = lay.DH if lay is L0 else D
                groups = KT * D // length
                for v in range(2):
                    link(nc.vector.tensor_tensor(
                        wprod.rearrange("p (g l) -> p g l", l=length),
                        w_proj[:, i, :, :].rearrange("p k n -> p (k n)").rearrange("p (g l) -> p g l", l=length),
                        a_bc[:, 2 * i + v, 0:length].unsqueeze(1).broadcast_to([P, groups, length]), ALU.mult))
                    last = nc.vector.tensor_reduce(
                        wa[:, i, :, v * lay.H:(v + 1) * lay.H],
                        wprod.rearrange("p (k h d) -> p k h d", k=KT, d=lay.DH), X, ALU.add)
                    if v == 0:
                        link(last)
                    else:
                        last.then_inc(S[lay.name, "wa_made"], 1)

            def copy_scores(lay, c):
                n = lay.name
                dve.wait_ge(S[n, "scores_ready"], c + 1)
                nc.vector.tensor_copy(scT[0:2 * lay.H, c * 512:(c + 1) * 512], psum[0:2 * lay.H, 7, :])\
                    .then_inc(S[n, "scores_copied"], 1)

            def factors(lay):
                n, H = lay.name, lay.H
                dve.wait_ge(S[n, "ab_ready"], 1)
                link(nc.vector.tensor_copy(ab[:, 0:T * 2 * H], psum[:, 3, 0:T * 2 * H]))
                a_v, b_v = abv(lay)[:, :, 0:H], abv(lay)[:, :, H:2 * H]
                nc.vector.tensor_reduce(bmax_part[:, 0:H], b_v.rearrange("p t h -> p h t"), X, ALU.max)\
                    .then_inc(S[n, "bmax_part_made"], 1)
                thr_t = thrv(lay).rearrange("p h m t -> p m t h")
                nc.vector.tensor_scalar(thr_t[:, 0], b_v, BIG, TIE, ALU.mult, ALU.add)
                link(nc.vector.tensor_scalar(thr_t[:, 1], b_v, -1.0, None, ALU.mult))
                dve.wait_ge(S[n, "bmax_made"], 1)
                tv = tmp[:, 0:T * H].rearrange("p (t h) -> p t h", t=T)
                tw = tmp2[:, 0:T * H].rearrange("p (t h) -> p t h", t=T)
                bm = bmax[:, 0:H].unsqueeze(1).broadcast_to([P, T, H])
                nc.vector.tensor_tensor(tv, b_v, bm, ALU.subtract)
                link(nc.vector.tensor_tensor(tw, a_v, bm, ALU.add))
                nc.vector.tensor_scalar(bb(lay)[:, :, :, 0], tv, 1.0, LIFT, ALU.mult, ALU.add)
                nc.vector.tensor_scalar(bb(lay)[:, :, :, 1], tv, 0.2, LIFT, ALU.mult, ALU.add)\
                    .then_inc(S[n, "exps_ready"], 1)
                w_t = wv(lay).rearrange("p h t m -> p m t h")
                nc.vector.tensor_scalar(w_t[:, 0], tw, 0.8, 0.0, ALU.mult, ALU.min)
                nc.vector.tensor_scalar(w_t[:, 1], tw, -0.8, 0.0, ALU.mult, ALU.min)\
                    .then_inc(S[n, "exps_ready"], 1)

            def convert_adj(t):
                s = t % ADJ_SLOTS
                dve.wait_ge(adj_in_done[s], 16 * (t // ADJ_SLOTS + 1))
                nc.vector.tensor_scalar(near8[:, t, :], adj_in[:, s, :], 0.0, -1.0, ALU.is_gt, ALU.mult,
                                        saturate=False).then_inc(adj_made, 1)

            def attention(lay):
                n = lay.name
                mine, theirs = lay.vector_tiles, lay.scalar_tiles
                SB, UH = lay.SB, lay.UH

                def thresholds(q, s):
                    nc.vector.tensor_copy(
                        thr_unit[:, s % 2, :, :],
                        thrv(lay)[:, ds(lay.head(q, s), 1), :, :].rearrange("p o m t -> p (o m) t"))\
                        .then_inc(S[n, "thr_made"], 1)

                def build(head, slot, g, made, step):
                    tiles = slice(g * lay.PT, (g + 1) * lay.PT)
                    dst = pack(lay, slot)[:, tiles]
                    if step == 0:
                        if not (isinstance(made, int) and made == 1):
                            dve.wait_ge(S[n, "lo_made"], made - 1)
                        b_h = bb(lay)[:, tiles, ds(head, 1), :].rearrange("p t o m -> p t (o m)")
                        v_h = vals[:, tiles, ds(head * lay.DH, lay.DH)]
                        nc.vector.tensor_tensor(
                            prodv(lay)[:, :, :, 0:lay.DH],
                            v_h.unsqueeze(2).broadcast_to([P, lay.PT, 2, lay.DH]),
                            b_h.unsqueeze(3).broadcast_to([P, lay.PT, 2, lay.DH]), ALU.mult)
                        nc.vector.tensor_copy(prodv(lay)[:, :, :, lay.DH], b_h)\
                            .then_inc(S[n, "x_made"], 1)
                    elif step == 1:
                        dve.wait_ge(S[n, "hi_made"], made)
                        nc.vector.tensor_tensor(prodv(lay), prodv(lay), dst[:, :, :, 0, :], ALU.subtract)\
                            .then_inc(S[n, "r_made"], 1)
                    else:
                        dve.wait_ge(S[n, "mid_made"], made)
                        nc.vector.tensor_tensor(dst[:, :, :, 2, :], prodv(lay), dst[:, :, :, 1, :],
                                                ALU.subtract).then_inc(S[n, "lo_made"], 1)

                def mask(q, s, t):
                    slot = t % MASK_SLOTS
                    first = isinstance(q, int) and q == 0 and s == 0
                    if t in mine:
                        last_tile = T * s + (mine[mine.index(t) - 1] - (T if t == mine[0] else 0))
                        dve.wait_ge(S[n, "masks_made"], T * SB * q + (last_tile + 1 + MASKS0))
                        dve.sem_inc(dve_gate, 1)
                    if t < MASK_SLOTS and t + MASK_SLOTS >= FREED:
                        if not first:
                            dve.wait_ge(S[n, "acc_ready"], BANKS * SB * q + BANKS * s)
                    else:
                        done = max(BLOCK, t - MASK_SLOTS + 1) if t >= MASK_SLOTS \
                            else t + MASK_SLOTS + 1 - FREED
                        dve.wait_ge(S[n, "mask_slots_free"],
                                    SB * FREED * q + (FREED * s + done + MASK_SLOTS))
                    if t in mine:
                        c = mine.index(t)
                        dve.sem_inc(dve_gate, 1)
                        nc.vector.tensor_scalar(step_v[:, 0:lay.W], row(lay, s % 2),
                                                thr_unit[:, s % 2, 1, t:t + 1],
                                                None, ALU.is_ge, saturate=False)\
                            .then_inc(S[n, "compare_made"], 1)
                        dve.wait_ge(S[n, "compare_made"], SB * len(mine) * q + (len(mine) * s + c + 1))
                        src = step_v[:, 0:lay.W]
                    else:
                        c = theirs.index(t)
                        dve.wait_ge(S[n, "step_made"], SB * len(theirs) * q + (len(theirs) * s + c + 1))
                        src = steps[:, lay.step_slot[c + s * len(theirs)], 0:lay.W]
                    last = nc.vector.tensor_tensor(masks(lay, slot, 0).bitcast(u32), src.bitcast(u32),
                                                   near(lay, s, t).bitcast(u32), ALU.bitwise_and)
                    if t not in lay.whole_tiles:
                        last = nc.vector.scalar_tensor_tensor(
                            out=masks(lay, slot, 1).bitcast(u32), in0=src.bitcast(u32), scalar=MINUS8,
                            in1=near(lay, s, t).bitcast(u32), op0=ALU.bitwise_xor, op1=ALU.bitwise_and)
                    last.then_inc(S[n, "masks_made"], 1)

                c = PARTS * lay.C
                per = lay.per_bank * 2

                def drain_bank(q, s, b):
                    dve.wait_ge(S[n, "acc_ready"], SB * BANKS * q + (BANKS * s + b + 1))
                    nc.vector.tensor_reduce(
                        num[:, b * per * lay.C:(b + 1) * per * lay.C].rearrange("p (g c) -> p g c", c=lay.C),
                        psum[:, b, 0:per * c].rearrange("p (g r c) -> p g c r", g=per, r=PARTS),
                        X, ALU.add).then_inc(S[n, "acc_free"], 1)

                def normalise(q, s, step):
                    size = lay.NI * lay.C
                    nv = num[:, 0:2 * size].rearrange("p (t m c) -> p t m c", t=lay.NI, m=2)
                    dn = den[:, 0:size].rearrange("p (t c) -> p t c", t=lay.NI)
                    rc = rec[:, 0:lay.NI]
                    tiles = slice(lay.half(s) * lay.NI, (lay.half(s) + 1) * lay.NI)
                    if step == 0:
                        dve.wait_ge(S[n, "acc_free"], SB * BANKS * q + (BANKS * s + 2 * BANKS))
                        w = wv(lay)[:, ds(lay.head(q, s), 1), tiles, :].rearrange("p o t m -> p (o t) m")
                        nc.vector.tensor_tensor(nv, nv, w.unsqueeze(3).broadcast_to([P, lay.NI, 2, lay.C]),
                                                ALU.mult).then_inc(S[n, "norm_order"], 1)
                        return
                    dve.wait_ge(S[n, "norm_order"], 3 * SB * q + (3 * s + step))
                    if step == 1:
                        nc.vector.tensor_tensor(dn, nv[:, :, 0, :], nv[:, :, 1, :], ALU.subtract)\
                            .then_inc(S[n, "norm_order"], 1)
                    elif step == 2:
                        nc.vector.reciprocal(rc, dn[:, :, lay.DH]).then_inc(S[n, "norm_order"], 1)
                    else:
                        nc.vector.tensor_tensor(
                            feat[:, tiles, ds(lay.head(q, s) * lay.DH, lay.DH)],
                            dn[:, :, 0:lay.DH], rc.unsqueeze(2).broadcast_to([P, lay.NI, lay.DH]),
                            ALU.mult).then_inc(S[n, "hid_made"], 1)

                def unit(q, s, last=False):
                    first = isinstance(q, int) and q == 0 and s == 0
                    before = (q, s - 1) if s else (q - 1, SB - 1)
                    dve.wait_ge(S[n, f"row_loaded{s % 2}"], 16 * (SB // 2) * q + 16 * (s // 2 + 1))
                    share = s + UH
                    for t in range(T):
                        if t == AHEAD and not first:
                            for b in range(BANKS):
                                drain_bank(*before, b)
                        mask(q, s, t)
                        if not first and t in NORM_AT:
                            normalise(*before, NORM_AT.index(t))
                        if t == THR_AT and not (last and s == SB - 1):
                            thresholds(*((q, s + 1) if s + 1 < SB else (q + 1, 0)))
                        if t in BUILD_AT and not (last and share >= SB):
                            build(lay.head(q, share), lay.pack_slot(share), lay.half(s),
                                  SB * q + (s + 1 + UH), BUILD_AT.index(t))

                dve.sem_inc(S[n, "masks_made"], MASKS0)
                dve.sem_inc(S[n, "acc_free"], BANKS)
                dve.wait_ge(S[n, "exps_made"], 2)
                thresholds(0, 0)
                dve.wait_ge(S[n, "v_copied"], T)
                for g in range(UH):
                    for step in range(3):
                        build(0, 0, g, g + 1, step)
                dve.wait_ge(S[n, "thr_made"], 1)
                for s in range(SB):
                    unit(0, s)
                with dve.Fori(1, lay.Q - 1, 1) as q:
                    for s in range(SB):
                        unit(q, s)
                for s in range(SB):
                    unit(lay.Q - 1, s, True)
                for b in range(BANKS):
                    drain_bank(lay.Q - 1, SB - 1, b)
                for step in range(4):
                    normalise(lay.Q - 1, SB - 1, step)

            scores_of_weights(L0, 0)
            for c in range(4):
                copy_scores(L0, c)
                for t in ((0,), (1, 2), (3, 4), (5, 6))[c]:
                    convert_adj(t)
            factors(L0)
            for t in range(7, 10):
                convert_adj(t)
            scores_of_weights(L1, 1)
            for t in range(10, T):
                convert_adj(t)
            attention(L0)

            dve.wait_ge(const_in, 64)

            def y_of(t):
                dve.wait_ge(o_ready, t + 1)
                nc.vector.tensor_tensor(yb[:, t % 2, :], psum[:, 2 + t % 2, :], b_out_sb[:, :], ALU.add)\
                    .then_inc(y_made, 1)
                dve.wait_ge(y_made, t + 1)
                nc.vector.tensor_scalar(eb[:, t % 2, :], yb[:, t % 2, :], 0.0, None, ALU.min)\
                    .then_inc(m_made, 1)

            def stat(t):
                link(nc.vector.bn_stats(stats[:, t % 2, :], resid[:, t, :]))
                return nc.vector.bn_aggr(mv[:, t, :], stats[:, t % 2, :])

            def z_of(t):
                s = t % 2
                dve.wait_ge(e_made, t + 1)
                nc.vector.scalar_tensor_tensor(out=eb[:, s, :], in0=eb[:, s, :], scalar=-1.0, in1=yb[:, s, :],
                                               op0=ALU.add, op1=ALU.max).then_inc(z_order, 1)
                dve.wait_ge(z_order, t + 1)
                dve.wait_ge(resid_in[s], 16 * (t // 2 + 1))
                link(nc.vector.tensor_tensor(resid[:, t, :], eb[:, s, :], resid[:, t, :], ALU.add))
                link(stat(t))

            def variances(g, made):
                nc.vector.tensor_scalar(std[:, 4 * g:4 * g + 4], mv[:, 4 * g:4 * g + 4, 1], EPS, None, ALU.add)\
                    .then_inc(made, 1)

            def normed(g, back, made):
                dve.wait_ge(back, g + 1)
                link(nc.vector.reciprocal(rstd[:, 4 * g:4 * g + 4], std[:, 4 * g:4 * g + 4]))
                for t in range(4 * g, 4 * g + 4):
                    nc.vector.tensor_scalar(resid[:, t, :], resid[:, t, :], mv[:, t, 0:1], rstd[:, t:t + 1],
                                            ALU.subtract, ALU.mult).then_inc(made, 1)

            for t in range(T + 1):
                if t < T:
                    y_of(t)
                if t >= 1:
                    z_of(t - 1)
                if t >= 4 and t % 4 == 0:
                    variances(t // 4 - 1, var_made)
                if t >= 5 and t % 4 == 1:
                    normed((t - 5) // 4, std_made, x1_made)
                if t >= 11 and t % 4 == 3:
                    copy_scores(L1, (t - 11) // 4)
            normed(3, std_made, x1_made)
            copy_scores(L1, 2)
            copy_scores(L1, 3)
            factors(L1)
            dve.wait_ge(x1_out, 16 * T)
            dve.wait_ge(x1_turned, T)
            attention(L1)

            def enc_min(t):
                if t >= 2:
                    dve.wait_ge(enc_made, t - 1)
                nc.vector.tensor_scalar(eb[:, t % 2, :], feat[:, t, :], 0.0, None, ALU.min)\
                    .then_inc(min_made, 1)

            def enc_end(t):
                dve.wait_ge(exp_made, t + 1)
                nc.vector.scalar_tensor_tensor(out=feat[:, t, :], in0=eb[:, t % 2, :], scalar=-1.0,
                                               in1=feat[:, t, :], op0=ALU.add, op1=ALU.max)\
                    .then_inc(enc_made, 1)

            def enc(c):
                for t in range(4 * c, 4 * c + 4):
                    enc_min(t)
                    if t > 4 * c:
                        enc_end(t - 1)
                enc_end(4 * c + 3)

            def final(t):
                s = t % 2
                dve.wait_ge(f_ready, t + 1)
                nc.vector.tensor_tensor(yb[:, s, :], psum[:, 7 if s else 6, :], b4_sb, ALU.add)\
                    .then_inc(f_read, 1)
                dve.wait_ge(f_read, t + 1)
                dve.wait_ge(x1_back[s], 16 * (t // 2 + 1))
                link(nc.vector.tensor_tensor(resid[:, t, :], yb[:, s, :], resid[:, t, :], ALU.add))
                link(stat(t))

            dve.wait_ge(S["l1", "hid_made"], UNITS)
            dve.wait_ge(net_in, 80)
            enc(0)
            for c in range(5):
                if c < 3:
                    enc(c + 1)
                if c >= 1:
                    for t in range(4 * c - 4, 4 * c):
                        final(t)
                    variances(c - 1, var2_made)
                if c >= 2:
                    normed(c - 2, std2_made, out_made)
            normed(3, std2_made, out_made)

        @block.tensor
        def _(pe):
            def score_chunk(lay, c):
                i = LAYERS.index(lay)
                if c:
                    pe.wait_ge(S[lay.name, "scores_copied"], c)
                for k in range(KT):
                    last = nc.tensor.matmul(psum[0:2 * lay.H, 7, :].rearrange("p (t n) -> p t n", t=4),
                                            wa[:, i, k, 0:2 * lay.H], featT[:, 4 * c:4 * c + 4, k, :],
                                            start=(k == 0), stop=(k == KT - 1))
                last.then_inc(S[lay.name, "scores_ready"], 1)

            def turn_scores(lay):
                H = lay.H
                pe.wait_ge(S[lay.name, "scores_copied"], 4)
                for t in range(T):
                    last = nc.tensor.transpose(psum[:, 3, t * 2 * H:(t + 1) * 2 * H],
                                               scT[0:2 * H, t * P:(t + 1) * P], ident[0:2 * H, 0:2 * H])
                last.then_inc(S[lay.name, "ab_ready"], 1)

            def v_of(lay, t):
                i = LAYERS.index(lay)
                ahead = 3 if lay is L0 else 1 if t < 12 else 2
                if t >= ahead and not (lay is L1 and t in (12, 13)):
                    pe.wait_ge(S[lay.name, "v_copied"], t - ahead + 1)
                for k in range(KT):
                    last = nc.tensor.matmul(psum[:, v_bank(lay, t), :], featT[:, t, k, :],
                                            w_proj[:, i, k, :], start=(k == 0), stop=(k == KT - 1))
                last.then_inc(S[lay.name, "v_ready"], 1)

            def attention(lay):
                n = lay.name
                SB = lay.SB
                pe.wait_ge(S[n, "v_copied"], T)
                pe.wait_ge(S[n, "bmax_part_made"], 1)
                pe.sem_inc(S[n, "mask_slots_free"], MASK_SLOTS)

                def masks_wait(q, s, t):
                    pe.wait_ge(S[n, "masks_made"],
                               T * SB * q + (T * s + t + 1 + MASKS0))
                    pe.sem_inc(pe_gate, 1)

                def products(s, t, it):
                    at = slice(it * P, (it + 1) * P)
                    first = t == 0 and it % lay.per_bank == 0
                    src = pack(lay, lay.pack_slot(s))[:, t].rearrange("p m r c -> p m (r c)")
                    if t in lay.whole_tiles:
                        nc.tensor.matmul(bank_out(lay, it, 0, 2),
                                         masks(lay, t % MASK_SLOTS, 0)[:, at],
                                         src.rearrange("p m c -> p (m c)"),
                                         start=first, stop=(t == T - 1), skip_group_check=True)
                        return nc.tensor.matmul(bank_out(lay, it, 1, 2), near(lay, s, t)[:, at],
                                                src[:, 1, :], start=False, stop=(t == T - 1),
                                                skip_group_check=True)
                    for m in range(2):
                        last = nc.tensor.matmul(bank_out(lay, it, m, m + 1),
                                                masks(lay, t % MASK_SLOTS, m)[:, at], src[:, m, :],
                                                start=(first and m == 0), stop=(t == T - 1),
                                                skip_group_check=True)
                    return last

                with pe.Fori(0, lay.Q, 1) as q:
                    for s in range(SB):
                        pe.wait_ge(S[n, "lo_made"], SB * q + lay.UH * (s // lay.UH + 1))
                        pe.sem_inc(pe_gate, 1)
                        masks_wait(q, s, BLOCK - 1)
                        for b in range(BANKS):
                            pe.wait_ge(S[n, "acc_free"], SB * BANKS * q + (BANKS * s + b + 1))
                            pe.sem_inc(pe_gate, 1)
                            for t in range(BLOCK):
                                for it in range(b * lay.per_bank, (b + 1) * lay.per_bank):
                                    last = products(s, t, it)
                        last.then_inc(S[n, "mask_slots_free"], BLOCK)
                        for t in range(BLOCK, T - BLOCK):
                            masks_wait(q, s, t)
                            for it in range(lay.NI):
                                last = products(s, t, it)
                            last.then_inc(S[n, "mask_slots_free"], 1)
                        masks_wait(q, s, T - 1)
                        for b in range(BANKS):
                            for t in range(T - BLOCK, T):
                                for it in range(b * lay.per_bank, (b + 1) * lay.per_bank):
                                    last = products(s, t, it)
                            last.then_inc(S[n, "acc_ready"], 1)

            def turn(t, bank, src):
                for k in range(KT):
                    last = nc.tensor.transpose(psum[:, bank, k * P:(k + 1) * P],
                                               src[:, t, k * P:(k + 1) * P], ident[:, :])
                return last

            pe.wait_ge(w_in[0], 16)
            pe.wait_ge(x_in[0], 16)
            v_of(L0, 0)
            v_of(L0, 1)
            pe.wait_ge(S["l0", "wa_made"], 1)
            for c in range(4):
                if c:
                    pe.wait_ge(x_in[c], 16)
                score_chunk(L0, c)
                v_of(L0, 2 + c)
            pe.wait_ge(ident_step, 2)
            turn_scores(L0)
            for t in range(6, T):
                v_of(L0, t)
            attention(L0)

            pe.wait_ge(S["l0", "hid_made"], UNITS)
            pe.wait_ge(S["l0", "acc_free"], BANKS * UNITS + BANKS)
            pe.wait_ge(w_in[2], 16)
            for t in range(-1, T + 6):
                if 0 <= t + 1 < T:
                    if t >= 1:
                        pe.wait_ge(h_copied, t)
                    turn(t + 1, (t + 1) % 2, feat).then_inc(h_turned, 1)
                if 0 <= t < T:
                    pe.wait_ge(h_copied, t + 1)
                    if t >= 2:
                        pe.wait_ge(y_made, t - 1)
                    for k in range(KT):
                        last = nc.tensor.matmul(psum[:, 2 + t % 2, :], hT[:, t % 2, k, :],
                                                w_proj[:, 0, k, :], start=(k == 0), stop=(k == KT - 1))
                    last.then_inc(o_ready, 1)
                if 0 <= t - 6 < T:
                    pe.wait_ge(x1_made, t - 5)
                    if t >= 8:
                        pe.wait_ge(x1_copied, t - 7)
                    turn(t - 6, 4 + (t - 6) % 2, resid).then_inc(x1_turned, 1)
                if 0 <= t - 7 < 12:
                    pe.wait_ge(x1_copied, t - 6)
                    v_of(L1, t - 7)
                    if (t - 7) % 4 == 3:
                        score_chunk(L1, (t - 7) // 4)
            pe.wait_ge(x1_copied, T)
            score_chunk(L1, 3)
            v_of(L1, 12)
            pe.wait_ge(y_made, T)
            turn_scores(L1)
            for t in range(13, T):
                v_of(L1, t)
            attention(L1)

            pe.wait_ge(S["l1", "acc_free"], BANKS * UNITS + BANKS)
            pe.wait_ge(net_in, 80)

            def turn_enc(t):
                pe.wait_ge(enc_made, t + 1)
                if t >= 2:
                    pe.wait_ge(e_copied, t - 1)
                turn(t, t % 2, feat).then_inc(e_turned, 1)

            def out_of(t):
                if t >= 2:
                    pe.wait_ge(f_read, t - 1)
                for k in range(2):
                    last = nc.tensor.matmul(psum[:, 7 if t % 2 else 6, :],
                                            h3T[:, k, t % 4 * P:(t % 4 + 1) * P], w4_sb[:, k, :],
                                            start=(k == 0), stop=(k == 1))
                last.then_inc(f_ready, 1)

            for t in range(4):
                turn_enc(t)
            for c in range(4):
                pe.wait_ge(e_copied, 4 * c + 4)
                for f in range(2):
                    if c >= 1:
                        pe.wait_ge(h_made, 5 * c - 5 + f + 1)
                    for k in range(KT):
                        last = nc.tensor.matmul(psum[:, 2 + f, :], w1_sb[:, k, f * P:(f + 1) * P],
                                                encT[:, c % 2, k, :], start=(k == 0), stop=(k == KT - 1))
                    last.then_inc(h_ready, 1)
                if c >= 1:
                    for t in range(4 * c - 4, 4 * c - 2):
                        out_of(t)
                pe.wait_ge(h_made, 5 * c + 2)
                for k in range(2):
                    last = nc.tensor.matmul(psum[:, 4, :], w2_sb[:, k, :], h1T[:, k, :],
                                            start=(k == 0), stop=(k == 1))
                last.then_inc(h_ready, 1)
                if c < 3:
                    for t in range(4 * c + 4, 4 * c + 8):
                        turn_enc(t)
                if c >= 1:
                    for t in range(4 * c - 2, 4 * c):
                        out_of(t)
                pe.wait_ge(h_made, 5 * c + 3)
                for f in range(2):
                    nc.tensor.matmul(psum[:, 4 if f else 5, :], w3_sb[:, f * P:(f + 1) * P], h2T,
                                     start=True, stop=True).then_inc(h_ready, 1)
                pe.wait_ge(h_made, 5 * c + 5)
            for t in range(12, 16):
                out_of(t)


def kernel(x, adj, L0_gnn_W_seq, L0_gnn_a1, L0_gnn_a2, L0_gnn_W_out, L0_gnn_b_out, L1_gnn_W, L1_gnn_a1,
           L1_gnn_a2, L1_gnn_W1, L1_gnn_b1, L1_gnn_W2, L1_gnn_b2, L1_gnn_W3, L1_gnn_b3, L1_gnn_W4, L1_gnn_b4):
    import numpy as np
    import concourse.bacc as bacc
    from concourse import mybir as mb
    from concourse.bass_utils import run_bass_kernel_spmd

    def flat(a, *shape):
        return np.ascontiguousarray(np.asarray(a)).reshape(*shape)

    def turned(a):
        return np.ascontiguousarray(np.asarray(a).T)

    def columns(a, n):
        return np.ascontiguousarray(np.asarray(a).reshape(n, 128).T)

    nc = bacc.Bacc("TRN2", target_bir_lowering=False, num_devices=1)
    arrays = {
        "xT": np.ascontiguousarray(np.asarray(x).reshape(T, 128, KT, 128).transpose(3, 0, 2, 1))
        .reshape(128, 4, -1),
        "x": flat(x, N, D), "adjT": turned(adj),
        "w_seq": flat(L0_gnn_W_seq, D, D), "a1_0": flat(L0_gnn_a1, 1, -1), "a2_0": flat(L0_gnn_a2, 1, -1),
        "w_out": flat(L0_gnn_W_out, D, D), "b_out": flat(L0_gnn_b_out, 1, D),
        "w_heads": np.ascontiguousarray(np.asarray(L1_gnn_W).transpose(1, 0, 2)).reshape(D, D),
        "a1_1": flat(L1_gnn_a1, 1, D), "a2_1": flat(L1_gnn_a2, 1, D),
        "w1T": turned(L1_gnn_W1), "b1": columns(L1_gnn_b1, 2),
        "w2T": turned(L1_gnn_W2), "b2": columns(L1_gnn_b2, 1),
        "w3T": turned(L1_gnn_W3), "b3": columns(L1_gnn_b3, 2),
        "w4T": turned(L1_gnn_W4), "b4": flat(L1_gnn_b4, 1, D),
    }
    args = [nc.dram_tensor(n, a.shape, mb.dt.from_np(a.dtype), kind="ExternalInput").ap()
            for n, a in arrays.items()]
    out = nc.dram_tensor("out", (T, P, D), mb.dt.float32, kind="ExternalOutput").ap()
    rows = nc.dram_tensor("rows", (16, N), mb.dt.float32).ap()
    x1_keep = nc.dram_tensor("x1_keep", (T, P, D), mb.dt.float32).ap()
    gat_kernel(nc, *args, out, rows, x1_keep)
    r = run_bass_kernel_spmd(nc, [arrays], core_ids=[0])
    return r.results[0]["out"].reshape(N, D)
```

```python
from contextlib import ExitStack

import concourse.bass as bass
from concourse import mybir

ds = bass.ds

P = 128
N = 2048
D = 512
T = N // P
KT = D // P
PARTS = 3
UNITS = 16
MASK_SLOTS = 8
STEP_SLOTS = 6
AHEAD = 3
NORM_AT = (6, 8, 10, 12)
THR_AT, HIGH_AT, MIDDLE_AT, BUILD_AT = 9, 10, 13, (4, 11, 15)
X1_LAG = 7
BANKS = 8
FIRST_PARTS = (slice(0, T // 2), slice(T // 2, T - 2), slice(T - 2, T))
FIRST_SHARES = len(FIRST_PARTS)
EARLY = 3
ADJ_SLOTS = 4
MASKS0 = 2 * T
BIG = 2.0 ** 80
TIE = 60.0
MINUS8 = 0xB8B8B8B8
LIFT = 64.0
EPS = 1e-5
GROUPS = (0, 4, 8, 12, 16)
GROUPS2 = (0, 4, 8, 12, 14, 16)


def slot_rounds(count, slots):
    rounds = -(-count // slots)
    slot = [i for r in range(rounds) for i in range(count // rounds + (r < count % rounds))]
    last = [max(j for j in range(i - count, i) if slot[j % count] == slot[i]) for i in range(count)]
    return slot, last


class Layer:

    def __init__(self, name, heads, body_units, vector_tiles, whole_tiles):
        self.name = name
        self.H = heads
        self.DH = D // heads
        self.C = self.DH + 1
        self.W = heads * N // UNITS
        self.NI = self.W // P
        self.per_bank = self.NI // BANKS
        self.UH = UNITS // heads
        self.PT = T // self.UH
        self.TILE = 2 * PARTS * self.C
        self.SB = body_units
        self.Q = UNITS // body_units
        self.vector_tiles = vector_tiles
        self.whole_tiles = whole_tiles
        self.scalar_tiles = [t for t in range(T) if t not in vector_tiles]
        self.step_slot, self.step_last = slot_rounds(len(self.scalar_tiles) * body_units, STEP_SLOTS)

    def head(self, q, s):
        return self.SB // self.UH * q + s // self.UH

    def pack_slot(self, s):
        return s // self.UH % 2

    def share(self, s):
        return slice(self.half(s) * self.PT, (self.half(s) + 1) * self.PT)

    def half(self, s):
        return s % self.UH


L0 = Layer("l0", 16, 2, (4, 9, 14), (0, 2, 4, 6, 8, 10, 12, 14))
L1 = Layer("l1", 8, 4, (), ())
LAYERS = (L0, L1)


def gat_kernel(nc, xT, x, adjT, w_seq, a1_0, a2_0, w_out, b_out, w_heads, a1_1, a2_1,
               w1T, b1, w2T, b2, w3T, b3, w4T, b4, out, rows, x1_keep):
    dt = mybir.dt
    ALU = mybir.AluOpType
    ACT = mybir.ActivationFunctionType
    X = mybir.AxisListType.X
    f32, bf16, f8, u32 = dt.float32, dt.bfloat16, dt.float8e4, dt.uint32
    RMAX = bass.bass_isa.ReduceOp.max

    ctx = ExitStack()
    with ctx:
        def sb(name, shape, dtype):
            return ctx.enter_context(nc.sbuf_tensor(name, shape, dtype))

        def sem(name):
            return ctx.enter_context(nc.semaphore(name))

        near8 = sb("near8", [P, T, N], f8)
        feat = sb("feat", [P, T, D], f32)
        featT = feat[:, :, :].rearrange("p t (k n) -> p t k n", k=KT)
        vals = sb("vals", [P, T, D], f32)
        w_proj = sb("w_proj", [P, 2, KT, D], f32)
        net_w = w_proj[:, :, :, :].rearrange("p i k n -> p (i k n)")
        w1_sb = net_w[:, 0:1024].rearrange("p (k n) -> p k n", k=KT)
        w4_sb = net_w[:, 1024:2048].rearrange("p (k n) -> p k n", k=2)
        w2_sb = net_w[:, 2048:2304].rearrange("p (k n) -> p k n", k=2)
        w3_sb = net_w[:, 2304:2560]
        b4_sb = net_w[:, 2560:3072]
        b_out_sb = sb("b_out_sb", [P, D], f32)
        b1_sb = sb("b1_sb", [P, 2], f32)
        b2_sb = sb("b2_sb", [P, 1], f32)
        b3_sb = sb("b3_sb", [P, 2], f32)
        ident = sb("ident", [P, P], f32)
        wa = sb("wa", [P, 2, KT, 32], f32)
        steps = sb("steps", [P, STEP_SLOTS, N], f8)
        before_steps = steps[:, STEP_SLOTS - 2:, :].rearrange("p s n -> p (s n)").bitcast(f32)
        ab = before_steps[:, 0:T * 32]
        tmp = before_steps[:, T * 32:T * 48]
        tmp2 = before_steps[:, T * 48:T * 64]
        bmax_part = sb("bmax_part", [P, 16], f32)
        bmax = sb("bmax", [P, 16], f32)
        BB = sb("BB", [P, T * 16 * 2], f32)
        ww = sb("ww", [P, T * 16 * 2], f32)
        thr = sb("thr", [P, T * 16 * 2], f32)
        thr_unit = sb("thr_unit", [P, 2, 2, T], f32)
        prod = sb("prod", [P, 1056], f32)
        step_v = sb("step_v", [P, N], f8)
        num = sb("num", [P, 1056], f32)
        den = sb("den", [P, 528], f32)
        rec = sb("rec", [P, T], f32)
        stats = sb("stats", [P, 2, 6], f32)
        mv = sb("mv", [P, T, 2], f32)
        std = sb("std", [P, T], f32)
        rstd = sb("rstd", [P, T], f32)

        RING0, ROW0 = 0, MASK_SLOTS * 2 * L0.W
        PACK0 = ROW0 + 2 * 4 * L0.W
        RING1, ROW1 = 0, MASK_SLOTS * 2 * L1.W
        PACK1 = ROW1 + 2 * 4 * L1.W
        ARENA = PACK0 + 2 * 2 * T * L0.TILE
        ROW_AT = {"l0": ROW0, "l1": ROW1}
        PACK_AT = {"l0": PACK0, "l1": PACK1}
        arena = sb("arena", [P, ARENA // 4], f32)
        flat = arena[:, :]
        adj_in = flat[:, 0:ADJ_SLOTS * N].rearrange("p (s n) -> p s n", s=ADJ_SLOTS)
        wprod = flat[:, ROW0 // 4:ROW0 // 4 + N]
        a_bc = flat[:, ROW0 // 4 + N:ROW0 // 4 + 2 * N].rearrange("p (v n) -> p v n", v=4)
        resid = flat[:, 0:T * D].rearrange("p (t d) -> p t d", t=T)
        scT = flat[0:32, 13312:13312 + N]
        TMP = T * D
        yb = flat[:, TMP:TMP + 2 * D].rearrange("p (s d) -> p s d", s=2)
        eb = flat[:, TMP + 2 * D:TMP + 4 * D].rearrange("p (s d) -> p s d", s=2)
        hT = flat[:, TMP + 4 * D:TMP + 6 * D].rearrange("p (s k n) -> p s k n", s=2, k=KT)
        h1T = flat[:, TMP + 4 * D:TMP + 6 * D].rearrange("p (f n) -> p f n", f=2)
        h2T = flat[:, TMP + 6 * D:TMP + 7 * D]
        h3T = flat[:, TMP + 7 * D:TMP + 9 * D].rearrange("p (f n) -> p f n", f=2)
        encT = vals[:, 0:8, :].rearrange("p (s k) n -> p s k n", s=2)

        psum = ctx.enter_context(nc.psum_tensor("psum", [P, BANKS, 512], f32))

        x_in = [sem(f"x_in_{c}") for c in range(4)]
        w_in = [sem(f"w_in_{i}") for i in range(3)]
        a_in = [sem(f"a_in_{i}") for i in range(2)]
        const_in = sem("const_in")
        net_in = sem("net_in")
        adj_in_done = [sem(f"adj_in_done_{i}") for i in range(ADJ_SLOTS)]
        adj_made = sem("adj_made")
        ident_step = sem("ident_step")
        dve_order = sem("dve_order")
        pe_gate = sem("pe_gate")
        act_gate = sem("act_gate")
        dve_gate = sem("dve_gate")
        S = {}
        for lay in LAYERS:
            for what in ("wa_made", "scores_ready", "scores_copied", "ab_ready", "bmax_part_made",
                         "bmax_made", "exps_ready", "exps_made", "a_rows_out",
                         "v_ready", "v_copied", "x_made", "hi_made", "r_made", "mid_made", "lo_made",
                         "row_loaded0", "row_loaded1", "thr_made", "step_made",
                         "compare_made", "masks_made", "mask_slots_free", "acc_ready", "acc_free",
                         "norm_order", "hid_made"):
                S[lay.name, what] = sem(f"{lay.name}_{what}")
        resid_in = [sem(f"resid_in_{i}") for i in range(2)]
        h_turned = sem("h_turned")
        h_copied = sem("h_copied")
        o_ready = sem("o_ready")
        y_made = sem("y_made")
        m_made = sem("m_made")
        e_made = sem("e_made")
        z_order = sem("z_order")
        var_made = sem("var_made")
        std_made = sem("std_made")
        x1_made = sem("x1_made")
        x1_turned = sem("x1_turned")
        x1_copied = sem("x1_copied")
        x1_out = sem("x1_out")
        x1_back = [sem(f"x1_back_{i}") for i in range(2)]
        min_made = sem("min_made")
        exp_made = sem("exp_made")
        enc_made = sem("enc_made")
        e_turned = sem("e_turned")
        e_copied = sem("e_copied")
        h_ready = sem("h_ready")
        h_made = sem("h_made")
        f_ready = sem("f_ready")
        f_read = sem("f_read")
        g_order = sem("g_order")
        var2_made = sem("var2_made")
        std2_made = sem("std2_made")
        out_made = sem("out_made")
        res_biased = sem("res_biased")
        out_done = sem("out_done")

        def bb(lay):
            return BB[:, 0:T * lay.H * 2].rearrange("p (t h m) -> p t h m", t=T, m=2)

        def wv(lay):
            return ww[:, 0:T * lay.H * 2].rearrange("p (h t m) -> p h t m", t=T, m=2)

        def thrv(lay):
            return thr[:, 0:T * lay.H * 2].rearrange("p (h m t) -> p h m t", t=T, m=2)

        def abv(lay):
            return ab[:, 0:T * 2 * lay.H].rearrange("p (t c) -> p t c", t=T)

        def prodv(lay):
            return prod[:, 0:lay.PT * 2 * lay.C].rearrange("p (t m c) -> p t m c", t=lay.PT, m=2)

        def width(tiles):
            return tiles.stop - tiles.start

        def masks(lay, slot, m):
            o = (slot * 2 + m) * lay.W
            return flat.bitcast(f8)[:, o:o + lay.W]

        def row(lay, slot):
            o = ROW_AT[lay.name] // 4 + slot * lay.W
            return flat[:, o:o + lay.W]

        def pack(lay, slot):
            o = PACK_AT[lay.name] // 2 + slot * T * lay.TILE
            return flat.bitcast(bf16)[:, o:o + T * lay.TILE].rearrange(
                "p (t m r c) -> p t m r c", t=T, m=2, r=PARTS)

        def bank_out(lay, it, m0, m1):
            c = PARTS * lay.C
            o = (it % lay.per_bank) * 2 * c
            return psum[:, it // lay.per_bank, o + m0 * c:o + m1 * c]

        def near(lay, s, t):
            return near8[:, t, lay.half(s) * lay.W:(lay.half(s) + 1) * lay.W]

        def v_bank(lay, t):
            return ((4, 5, 6) if lay is L0 else (6, 0, 1))[t % 3]

        BLOCK = 3
        FREED = T - BLOCK

        block = ctx.enter_context(nc.Block())

        @block.sync
        def _(sp):
            def store_rows(lay):
                sp.wait_ge(S[lay.name, "scores_copied"], 4)
                sp.dma_start(rows[0:lay.H, :], scT[0:lay.H, :]).then_inc(S[lay.name, "a_rows_out"], 16)

            def load_row(lay, q, s):
                units = rows[0:lay.H, :].rearrange("h (g n) -> (h g) n", g=lay.UH)
                sp.dma_start(row(lay, s), units[ds(2 * q + s, 1), :].partition_broadcast(P))\
                    .then_inc(S[lay.name, f"row_loaded{s}"], 16)

            def later_rows(lay):
                with sp.Fori(1, UNITS // 2, 1) as q:
                    for s in range(2):
                        sp.wait_ge(S[lay.name, "masks_made"], 2 * T * q + (T * s - T + MASKS0))
                        load_row(lay, q, s)

            sp.dma_start(w_proj[:, 0, :, :], w_seq.rearrange("(k p) n -> p k n", p=P)).then_inc(w_in[0], 16)
            for v, src in enumerate((a1_0, a2_0)):
                sp.dma_start(a_bc[:, v, 0:L0.DH], src.partition_broadcast(P)).then_inc(a_in[0], 16)
            for c in range(4):
                sp.dma_start(featT[:, 4 * c:4 * c + 4, :, :].rearrange("p t k n -> p (t k n)"),
                             xT[:, c, :]).then_inc(x_in[c], 16)
            sp.dma_start(w_proj[:, 1, :, :], w_heads.rearrange("(k p) n -> p k n", p=P))\
                .then_inc(w_in[1], 16)
            for v, src in enumerate((a1_1, a2_1)):
                sp.dma_start(a_bc[:, 2 + v, :], src.partition_broadcast(P)).then_inc(a_in[1], 16)
            for t in range(T):
                if t >= ADJ_SLOTS:
                    sp.wait_ge(adj_made, t - ADJ_SLOTS + 1)
                sp.dma_start(adj_in[:, t % ADJ_SLOTS, :], adjT[t * P:(t + 1) * P, :])\
                    .then_inc(adj_in_done[t % ADJ_SLOTS], 16)
                if t == 7:
                    store_rows(L0)
                if t == 13:
                    sp.wait_ge(S["l1", "wa_made"], 1)
                    sp.wait_ge(S["l0", "a_rows_out"], 16)
                    load_row(L0, 0, 0)
            load_row(L0, 0, 1)
            for dst, src in ((b_out_sb[:, :], b_out.partition_broadcast(P)),
                             (b1_sb[:, :], b1), (b2_sb[:, :], b2), (b3_sb[:, :], b3)):
                sp.dma_start(dst, src).then_inc(const_in, 16)
            sp.wait_ge(S["l0", "v_ready"], T)
            sp.dma_start(w_proj[:, 0, :, :], w_out.rearrange("(k p) n -> p k n", p=P)).then_inc(w_in[2], 16)
            later_rows(L0)

            sp.wait_ge(S["l0", "acc_ready"], BANKS * UNITS)
            for t in range(T):
                if t >= 2:
                    sp.wait_ge(resid_in[t % 2], 16 * (t // 2))
                sp.dma_start(resid[:, t, :], x[t * P:(t + 1) * P, :]).then_inc(resid_in[t % 2], 16)
            with sp.Fori(0, T // 2, 1) as q:
                for s in range(2):
                    sp.wait_ge(x1_made, 2 * q + (s + 1))
                    sp.dma_start(x1_keep[ds(2 * q + s, 1), :, :].rearrange("o p d -> p (o d)"),
                                 resid[:, ds(2 * q + s, 1), :].rearrange("p o d -> p (o d)"))\
                        .then_inc(x1_out, 16)
            store_rows(L1)
            sp.wait_ge(x1_out, 16 * T)
            sp.wait_ge(x1_turned, T)
            sp.wait_ge(S["l1", "a_rows_out"], 16)
            for s in range(2):
                load_row(L1, 0, s)
            sp.wait_ge(S["l1", "v_ready"], T)
            for dst, src in ((w1_sb, w1T.rearrange("(k p) n -> p k n", p=P)),
                             (w2_sb, w2T.rearrange("(k p) n -> p k n", p=P)),
                             (w3_sb, w3T),
                             (w4_sb, w4T.rearrange("(k p) n -> p k n", p=P)),
                             (b4_sb, b4.partition_broadcast(P))):
                sp.dma_start(dst, src).then_inc(net_in, 16)
            later_rows(L1)

            sp.wait_ge(S["l1", "acc_ready"], BANKS * UNITS)
            for t in range(T):
                if t >= 2:
                    sp.wait_ge(x1_back[t % 2], 16 * (t // 2))
                sp.dma_start(resid[:, t, :], x1_keep[t, :, :]).then_inc(x1_back[t % 2], 16)
            with sp.Fori(0, T // 2, 1) as q:
                for s in range(2):
                    sp.wait_ge(out_made, 2 * q + (s + 1))
                    sp.dma_start(out[ds(2 * q + s, 1), :, :].rearrange("o p d -> p (o d)"),
                                 resid[:, ds(2 * q + s, 1), :].rearrange("p o d -> p (o d)"))\
                        .then_inc(out_done, 16)
            sp.wait_ge(out_done, 16 * T)

        @block.gpsimd
        def _(pool):
            nc.gpsimd.memset(ident[:, :], 0.0).then_inc(ident_step, 1)
            pool.wait_ge(ident_step, 1)
            nc.gpsimd.affine_select(out=ident[:, :], in_=ident[:, :], compare_op=ALU.not_equal, fill=1.0,
                                    base=0, pattern=[[-1, P]], channel_multiplier=1)\
                .then_inc(ident_step, 1)
            for lay in LAYERS:
                pool.wait_ge(S[lay.name, "bmax_part_made"], 1)
                nc.gpsimd.partition_all_reduce(bmax[:, 0:lay.H], bmax_part[:, 0:lay.H], P, RMAX)\
                    .then_inc(S[lay.name, "bmax_made"], 1)

        @block.scalar
        def _(act):
            def exps(lay):
                n = lay.name
                act.wait_ge(S[n, "exps_ready"], 2)
                nc.scalar.activation(BB[:, 0:T * lay.H * 2], BB[:, 0:T * lay.H * 2], ACT.Exp)\
                    .then_inc(S[n, "exps_made"], 1)
                nc.scalar.activation(ww[:, 0:T * lay.H * 2], ww[:, 0:T * lay.H * 2], ACT.Exp)\
                    .then_inc(S[n, "exps_made"], 1)

            def copy_v(lay, t):
                act.wait_ge(S[lay.name, "v_ready"], t + 1)
                nc.scalar.activation(vals[:, t, :], psum[:, v_bank(lay, t), :], ACT.Copy)\
                    .then_inc(S[lay.name, "v_copied"], 1)

            def high(lay, slot, tiles, n_made):
                act.wait_ge(S[lay.name, "x_made"], n_made)
                nc.scalar.activation(pack(lay, slot)[:, tiles, :, 0, :], prodv(lay)[:, 0:width(tiles)],
                                     ACT.Copy).then_inc(S[lay.name, "hi_made"], 1)

            def middle(lay, slot, tiles, n_made):
                act.wait_ge(S[lay.name, "r_made"], n_made)
                nc.scalar.activation(pack(lay, slot)[:, tiles, :, 1, :], prodv(lay)[:, 0:width(tiles)],
                                     ACT.Copy).then_inc(S[lay.name, "mid_made"], 1)

            def compares(lay, v_left):
                n = lay.name
                mine = lay.scalar_tiles

                def compare(q, s, c):
                    t = mine[c]
                    use = c + s * len(mine)
                    last = lay.step_last[use]
                    last_tile = last // len(mine) * T + mine[last % len(mine)]
                    act.wait_ge(S[n, "masks_made"],
                                T * lay.SB * q + (last_tile + 1 + MASKS0))
                    act.sem_inc(act_gate, 1)
                    nc.scalar.activation(steps[:, lay.step_slot[use], 0:lay.W],
                                         row(lay, s % 2), ACT.Sigmoid,
                                         bias=thr_unit[:, s % 2, 0, t:t + 1], scale=BIG, saturate=False)\
                        .then_inc(S[n, "step_made"], 1)

                def unit_in(q, s):
                    act.wait_ge(S[n, f"row_loaded{s % 2}"], 16 * (lay.SB // 2) * q + 16 * (s // 2 + 1))
                    act.wait_ge(S[n, "thr_made"], lay.SB * q + (s + 1))

                def unit(q, s, build, done=0):
                    if not done:
                        unit_in(q, s)
                    nxt = s + lay.UH
                    args = (lay, lay.pack_slot(nxt), lay.share(s), lay.SB * q + (s + 1 + FIRST_SHARES))
                    for c, t in enumerate(mine):
                        if c >= done:
                            compare(q, s, c)
                        if build and t == HIGH_AT:
                            if lay.half(s) == 0 and not (isinstance(q, int) and q == 0 and s == 0):
                                act.wait_ge(S[n, "acc_ready"], BANKS * lay.SB * q + BANKS * s)
                            high(*args)
                        if build and t == MIDDLE_AT:
                            middle(*args)

                def first_parts(i):
                    high(lay, 0, FIRST_PARTS[i], i + 1)
                    middle(lay, 0, FIRST_PARTS[i], i + 1)

                early = len([t for t in mine if t < EARLY])
                for t in v_left:
                    c = t - (T - 1 - early)
                    if c == 0:
                        first_parts(0)
                        unit_in(0, 0)
                    if 0 <= c < early:
                        compare(0, 0, c)
                    copy_v(lay, t)
                    if t == T - 2:
                        first_parts(1)
                first_parts(2)
                for s in range(lay.SB):
                    unit(0, s, True, early if s == 0 else 0)
                with act.Fori(1, lay.Q - 1, 1) as q:
                    for s in range(lay.SB):
                        unit(q, s, True)
                for s in range(lay.SB):
                    unit(lay.Q - 1, s, s < lay.SB - lay.UH)

            for t in range(8):
                copy_v(L0, t)
            exps(L0)
            act.wait_ge(S["l0", "a_rows_out"], 16)
            compares(L0, range(8, T))

            for t in range(-1, T + X1_LAG):
                if 0 <= t + 1 < T:
                    act.wait_ge(h_turned, t + 2)
                    nc.scalar.activation(hT[:, (t + 1) % 2, :, :],
                                         psum[:, (t + 1) % 2, :].rearrange("p (k n) -> p k n", k=KT),
                                         ACT.Copy).then_inc(h_copied, 1)
                if 0 <= t < T:
                    act.wait_ge(m_made, t + 1)
                    nc.scalar.activation(eb[:, t % 2, :], eb[:, t % 2, :], ACT.Exp).then_inc(e_made, 1)
                if t >= 5 and t % 4 == 1 and t <= T + 1:
                    g = t // 4 - 1
                    act.wait_ge(var_made, g + 1)
                    nc.scalar.activation(std[:, 4 * g:4 * g + 4], std[:, 4 * g:4 * g + 4], ACT.Sqrt)\
                        .then_inc(std_made, 1)
                if 0 <= t - X1_LAG < T:
                    act.wait_ge(x1_turned, t - X1_LAG + 1)
                    nc.scalar.activation(feat[:, t - X1_LAG, :], psum[:, 4 + (t - X1_LAG) % 2, :], ACT.Copy)\
                        .then_inc(x1_copied, 1)
                if 0 <= t - 14 < 8:
                    copy_v(L1, t - 14)
            for t in range(8, 11):
                copy_v(L1, t)
            exps(L1)
            act.wait_ge(S["l1", "a_rows_out"], 16)
            act.wait_ge(x1_out, 16 * T)
            compares(L1, range(11, T))

            def enc_exp(t):
                act.wait_ge(min_made, t + 1)
                nc.scalar.activation(yb[:, t % 2, :], yb[:, t % 2, :], ACT.Exp).then_inc(exp_made, 1)

            def enc_copy(t):
                act.wait_ge(e_turned, t + 1)
                nc.scalar.activation(encT[:, t // 4 % 2, :, t % 4 * P:(t % 4 + 1) * P],
                                     psum[:, t % 2, :].rearrange("p (k n) -> p k n", k=KT),
                                     ACT.Copy).then_inc(e_copied, 1)

            def relu(c, i, dst, bank, bias):
                act.wait_ge(h_ready, 5 * c + i + 1)
                nc.scalar.activation(dst, psum[:, bank, :], ACT.Relu, bias=bias).then_inc(h_made, 1)

            for t in range(4):
                enc_exp(t)
            for t in range(4):
                enc_copy(t)
            for c in range(4):
                more = c < 3
                n = 4 * c + 4
                if more:
                    for t in range(n, n + 4):
                        enc_exp(t)
                relu(c, 0, h1T[:, 0, :], 2, b1_sb[:, 0:1])
                relu(c, 1, h1T[:, 1, :], 3, b1_sb[:, 1:2])
                if more:
                    enc_copy(n)
                    enc_copy(n + 1)
                relu(c, 2, h2T, 4, b2_sb[:, 0:1])
                if more:
                    enc_copy(n + 2)
                    enc_copy(n + 3)
                relu(c, 3, h3T[:, 0, :], 5, b3_sb[:, 0:1])
                relu(c, 4, h3T[:, 1, :], 4, b3_sb[:, 1:2])
                if c >= 1:
                    act.wait_ge(var2_made, c)
                    nc.scalar.activation(std[:, 4 * c - 4:4 * c], std[:, 4 * c - 4:4 * c], ACT.Sqrt)\
                        .then_inc(std2_made, 1)
            for g in (3, 4):
                act.wait_ge(var2_made, g + 1)
                tiles = slice(*GROUPS2[g:g + 2])
                nc.scalar.activation(std[:, tiles], std[:, tiles], ACT.Sqrt).then_inc(std2_made, 1)

        @block.vector
        def _(dve):
            ordered = [0]

            def link(ins):
                ordered[0] += 1
                ins.then_inc(dve_order, 1)
                dve.wait_ge(dve_order, ordered[0])

            def scores_of_weights(lay, i, between=lambda: None):
                dve.wait_ge(w_in[i], 16)
                dve.wait_ge(a_in[i], 32)
                length = lay.DH if lay is L0 else D
                groups = KT * D // length
                for v in range(2):
                    link(nc.vector.tensor_tensor(
                        wprod.rearrange("p (g l) -> p g l", l=length),
                        w_proj[:, i, :, :].rearrange("p k n -> p (k n)").rearrange("p (g l) -> p g l", l=length),
                        a_bc[:, 2 * i + v, 0:length].unsqueeze(1).broadcast_to([P, groups, length]), ALU.mult))
                    last = nc.vector.tensor_reduce(
                        wa[:, i, :, v * lay.H:(v + 1) * lay.H],
                        wprod.rearrange("p (k h d) -> p k h d", k=KT, d=lay.DH), X, ALU.add)
                    if v == 0:
                        link(last)
                        between()
                    else:
                        last.then_inc(S[lay.name, "wa_made"], 1)

            def copy_scores(lay, c):
                n = lay.name
                dve.wait_ge(S[n, "scores_ready"], c + 1)
                nc.vector.tensor_copy(scT[0:2 * lay.H, c * 512:(c + 1) * 512], psum[0:2 * lay.H, 7, :])\
                    .then_inc(S[n, "scores_copied"], 1)

            def factors(lay):
                n, H = lay.name, lay.H
                dve.wait_ge(S[n, "ab_ready"], 1)
                link(nc.vector.tensor_copy(ab[:, 0:T * 2 * H], psum[:, 3, 0:T * 2 * H]))
                a_v, b_v = abv(lay)[:, :, 0:H], abv(lay)[:, :, H:2 * H]
                nc.vector.tensor_reduce(bmax_part[:, 0:H], b_v.rearrange("p t h -> p h t"), X, ALU.max)\
                    .then_inc(S[n, "bmax_part_made"], 1)
                thr_t = thrv(lay).rearrange("p h m t -> p m t h")
                nc.vector.tensor_scalar(thr_t[:, 0], b_v, BIG, TIE, ALU.mult, ALU.add)
                link(nc.vector.tensor_scalar(thr_t[:, 1], b_v, -1.0, None, ALU.mult))
                dve.wait_ge(S[n, "bmax_made"], 1)
                tv = tmp[:, 0:T * H].rearrange("p (t h) -> p t h", t=T)
                tw = tmp2[:, 0:T * H].rearrange("p (t h) -> p t h", t=T)
                bm = bmax[:, 0:H].unsqueeze(1).broadcast_to([P, T, H])
                nc.vector.tensor_tensor(tv, b_v, bm, ALU.subtract)
                link(nc.vector.tensor_tensor(tw, a_v, bm, ALU.add))
                nc.vector.tensor_scalar(bb(lay)[:, :, :, 0], tv, 1.0, LIFT, ALU.mult, ALU.add)
                nc.vector.tensor_scalar(bb(lay)[:, :, :, 1], tv, 0.2, LIFT, ALU.mult, ALU.add)\
                    .then_inc(S[n, "exps_ready"], 1)
                w_t = wv(lay).rearrange("p h t m -> p m t h")
                nc.vector.tensor_scalar(w_t[:, 0], tw, 0.8, 0.0, ALU.mult, ALU.min)
                nc.vector.tensor_scalar(w_t[:, 1], tw, -0.8, 0.0, ALU.mult, ALU.min)\
                    .then_inc(S[n, "exps_ready"], 1)

            def convert_adj(t):
                s = t % ADJ_SLOTS
                dve.wait_ge(adj_in_done[s], 16 * (t // ADJ_SLOTS + 1))
                nc.vector.tensor_scalar(near8[:, t, :], adj_in[:, s, :], 0.0, -1.0, ALU.is_gt, ALU.mult,
                                        saturate=False).then_inc(adj_made, 1)

            def enc_min(t):
                if t >= 2:
                    dve.wait_ge(enc_made, t - 1)
                nc.vector.tensor_scalar(yb[:, t % 2, :], feat[:, t, :], 0.0, None, ALU.min)\
                    .then_inc(min_made, 1)

            def enc_end(t):
                dve.wait_ge(exp_made, t + 1)
                nc.vector.scalar_tensor_tensor(out=feat[:, t, :], in0=yb[:, t % 2, :], scalar=-1.0,
                                               in1=feat[:, t, :], op0=ALU.add, op1=ALU.max)\
                    .then_inc(enc_made, 1)

            def enc(c):
                for t in range(4 * c, 4 * c + 4):
                    enc_min(t)
                    if t > 4 * c:
                        enc_end(t - 1)
                enc_end(4 * c + 3)

            def attention(lay, part):
                n = lay.name
                mine, theirs = lay.vector_tiles, lay.scalar_tiles
                SB, UH = lay.SB, lay.UH

                def thresholds(q, s):
                    nc.vector.tensor_copy(
                        thr_unit[:, s % 2, :, :],
                        thrv(lay)[:, ds(lay.head(q, s), 1), :, :].rearrange("p o m t -> p (o m) t"))\
                        .then_inc(S[n, "thr_made"], 1)

                def build(head, slot, tiles, made, step):
                    dst = pack(lay, slot)[:, tiles]
                    src = prodv(lay)[:, 0:width(tiles)]
                    if step == 0:
                        if not (isinstance(made, int) and made == 1):
                            dve.wait_ge(S[n, "lo_made"], made - 1)
                        b_h = bb(lay)[:, tiles, ds(head, 1), :].rearrange("p t o m -> p t (o m)")
                        v_h = vals[:, tiles, ds(head * lay.DH, lay.DH)]
                        nc.vector.tensor_tensor(
                            src[:, :, :, 0:lay.DH],
                            v_h.unsqueeze(2).broadcast_to([P, width(tiles), 2, lay.DH]),
                            b_h.unsqueeze(3).broadcast_to([P, width(tiles), 2, lay.DH]), ALU.mult)
                        nc.vector.tensor_copy(src[:, :, :, lay.DH], b_h)\
                            .then_inc(S[n, "x_made"], 1)
                    elif step == 1:
                        dve.wait_ge(S[n, "hi_made"], made)
                        nc.vector.tensor_tensor(src, src, dst[:, :, :, 0, :], ALU.subtract)\
                            .then_inc(S[n, "r_made"], 1)
                    else:
                        dve.wait_ge(S[n, "mid_made"], made)
                        nc.vector.tensor_tensor(dst[:, :, :, 2, :], src, dst[:, :, :, 1, :],
                                                ALU.subtract).then_inc(S[n, "lo_made"], 1)

                def compare(q, s, t):
                    last_tile = T * s + (mine[mine.index(t) - 1] - (T if t == mine[0] else 0))
                    dve.wait_ge(S[n, "masks_made"], T * SB * q + (last_tile + 1 + MASKS0))
                    dve.sem_inc(dve_gate, 1)
                    nc.vector.tensor_scalar(step_v[:, 0:lay.W], row(lay, s % 2),
                                            thr_unit[:, s % 2, 1, t:t + 1],
                                            None, ALU.is_ge, saturate=False)\
                        .then_inc(S[n, "compare_made"], 1)

                def mask(q, s, t):
                    slot = t % MASK_SLOTS
                    first = isinstance(q, int) and q == 0 and s == 0
                    fresh = first and t < MASK_SLOTS
                    if not fresh and t < MASK_SLOTS and t + MASK_SLOTS >= FREED:
                        dve.wait_ge(S[n, "acc_ready"], BANKS * SB * q + BANKS * s)
                    elif not fresh:
                        done = max(BLOCK, t - MASK_SLOTS + 1) if t >= MASK_SLOTS \
                            else t + MASK_SLOTS + 1 - FREED
                        dve.wait_ge(S[n, "mask_slots_free"],
                                    SB * FREED * q + (FREED * s + done + MASK_SLOTS))
                    if t in mine:
                        c = mine.index(t)
                        dve.wait_ge(S[n, "compare_made"], SB * len(mine) * q + (len(mine) * s + c + 1))
                        src = step_v[:, 0:lay.W]
                    else:
                        c = theirs.index(t)
                        dve.wait_ge(S[n, "step_made"], SB * len(theirs) * q + (len(theirs) * s + c + 1))
                        src = steps[:, lay.step_slot[c + s * len(theirs)], 0:lay.W]
                    last = nc.vector.tensor_tensor(masks(lay, slot, 0).bitcast(u32), src.bitcast(u32),
                                                   near(lay, s, t).bitcast(u32), ALU.bitwise_and)
                    if t not in lay.whole_tiles:
                        last = nc.vector.scalar_tensor_tensor(
                            out=masks(lay, slot, 1).bitcast(u32), in0=src.bitcast(u32), scalar=MINUS8,
                            in1=near(lay, s, t).bitcast(u32), op0=ALU.bitwise_xor, op1=ALU.bitwise_and)
                    last.then_inc(S[n, "masks_made"], 1)

                c = PARTS * lay.C
                per = lay.per_bank * 2

                def drain_bank(q, s, b):
                    dve.wait_ge(S[n, "acc_ready"], SB * BANKS * q + (BANKS * s + b + 1))
                    nc.vector.tensor_reduce(
                        num[:, b * per * lay.C:(b + 1) * per * lay.C].rearrange("p (g c) -> p g c", c=lay.C),
                        psum[:, b, 0:per * c].rearrange("p (g r c) -> p g c r", g=per, r=PARTS),
                        X, ALU.add).then_inc(S[n, "acc_free"], 1)

                def normalise(q, s, step, its=None, extra=0):
                    its = its or slice(0, lay.NI)
                    count = width(its)
                    size = lay.NI * lay.C
                    nv = num[:, 0:2 * size].rearrange("p (t m c) -> p t m c", t=lay.NI, m=2)[:, its]
                    dn = den[:, 0:size].rearrange("p (t c) -> p t c", t=lay.NI)[:, its]
                    rc = rec[:, its]
                    tiles = slice(lay.half(s) * lay.NI + its.start, lay.half(s) * lay.NI + its.stop)
                    if step == 0:
                        dve.wait_ge(S[n, "acc_free"],
                                    SB * BANKS * q + (BANKS * s + its.stop // lay.per_bank + BANKS))
                        w = wv(lay)[:, ds(lay.head(q, s), 1), tiles, :].rearrange("p o t m -> p (o t) m")
                        nc.vector.tensor_tensor(nv, nv, w.unsqueeze(3).broadcast_to([P, count, 2, lay.C]),
                                                ALU.mult).then_inc(S[n, "norm_order"], 1)
                        return
                    dve.wait_ge(S[n, "norm_order"], 3 * SB * q + (3 * s + step + extra))
                    if step == 1:
                        nc.vector.tensor_tensor(dn, nv[:, :, 0, :], nv[:, :, 1, :], ALU.subtract)\
                            .then_inc(S[n, "norm_order"], 1)
                    elif step == 2:
                        nc.vector.reciprocal(rc, dn[:, :, lay.DH]).then_inc(S[n, "norm_order"], 1)
                    else:
                        nc.vector.tensor_tensor(
                            feat[:, tiles, ds(lay.head(q, s) * lay.DH, lay.DH)],
                            dn[:, :, 0:lay.DH], rc.unsqueeze(2).broadcast_to([P, count, lay.DH]),
                            ALU.mult).then_inc(S[n, "hid_made"], 1)

                def unit(q, s, last=False):
                    first = isinstance(q, int) and q == 0 and s == 0
                    before = (q, s - 1) if s else (q - 1, SB - 1)
                    dve.wait_ge(S[n, f"row_loaded{s % 2}"], 16 * (SB // 2) * q + 16 * (s // 2 + 1))
                    share = s + UH
                    for t in range(EARLY if first else 0, T):
                        if t == AHEAD and not first:
                            for b in range(BANKS):
                                drain_bank(*before, b)
                        if t + 1 in mine:
                            compare(q, s, t + 1)
                        mask(q, s, t)
                        if not first and t in NORM_AT:
                            normalise(*before, NORM_AT.index(t))
                        if t == THR_AT and not (last and s == SB - 1):
                            thresholds(*((q, s + 1) if s + 1 < SB else (q + 1, 0)))
                        if t in BUILD_AT and not (last and share >= SB):
                            build(lay.head(q, share), lay.pack_slot(share), lay.share(s),
                                  SB * q + (s + 1 + FIRST_SHARES), BUILD_AT.index(t))

                if part == "start":
                    dve.sem_inc(S[n, "masks_made"], MASKS0)
                    dve.sem_inc(S[n, "acc_free"], BANKS)
                    dve.wait_ge(S[n, "exps_made"], 2)
                    thresholds(0, 0)
                    dve.wait_ge(S[n, "v_copied"], FIRST_PARTS[0].stop)
                    for step in range(3):
                        build(0, 0, FIRST_PARTS[0], 1, step)
                    return
                dve.wait_ge(S[n, "thr_made"], 1)
                dve.wait_ge(S[n, "row_loaded0"], 16)
                for t in range(EARLY):
                    mask(0, 0, t)
                for i in (1, 2):
                    dve.wait_ge(S[n, "v_copied"], FIRST_PARTS[i].stop)
                    for step in range(3):
                        build(0, 0, FIRST_PARTS[i], i + 1, step)
                for s in range(SB):
                    unit(0, s)
                with dve.Fori(1, lay.Q - 1, 1) as q:
                    for s in range(SB):
                        unit(q, s)
                for s in range(SB):
                    unit(lay.Q - 1, s, True)
                if lay is L1:
                    dve.wait_ge(S[n, "hid_made"], UNITS - 1)
                    enc(0)
                end = (lay.Q - 1, SB - 1)
                for i in range(2):
                    for b in range(i * BANKS // 2, (i + 1) * BANKS // 2):
                        drain_bank(*end, b)
                    for step in range(4):
                        normalise(*end, step, slice(i * lay.NI // 2, (i + 1) * lay.NI // 2), 3 * i)

            def convert(first, end):
                for t in range(first, end):
                    convert_adj(t)

            def second_scores():
                copy_scores(L0, 1)
                convert(0, 1)

            scores_of_weights(L0, 0)
            copy_scores(L0, 0)
            scores_of_weights(L1, 1, second_scores)
            copy_scores(L0, 2)
            convert(1, 4)
            copy_scores(L0, 3)
            convert(4, 7)
            factors(L0)
            convert(7, 13)
            attention(L0, "start")
            convert(13, T)
            dve.wait_ge(adj_made, T)
            attention(L0, "units")

            dve.wait_ge(const_in, 64)

            def y_of(t):
                dve.wait_ge(o_ready, t + 1)
                nc.vector.tensor_tensor(yb[:, t % 2, :], psum[:, 2 + t % 2, :], b_out_sb[:, :], ALU.add)\
                    .then_inc(y_made, 1)
                dve.wait_ge(y_made, t + 1)
                nc.vector.tensor_scalar(eb[:, t % 2, :], yb[:, t % 2, :], 0.0, None, ALU.min)\
                    .then_inc(m_made, 1)

            def stat(t):
                link(nc.vector.bn_stats(stats[:, t % 2, :], resid[:, t, :]))
                return nc.vector.bn_aggr(mv[:, t, :], stats[:, t % 2, :])

            def z_of(t):
                s = t % 2
                dve.wait_ge(e_made, t + 1)
                nc.vector.scalar_tensor_tensor(out=eb[:, s, :], in0=eb[:, s, :], scalar=-1.0, in1=yb[:, s, :],
                                               op0=ALU.add, op1=ALU.max).then_inc(z_order, 1)
                dve.wait_ge(z_order, t + 1)
                dve.wait_ge(resid_in[s], 16 * (t // 2 + 1))
                link(nc.vector.tensor_tensor(resid[:, t, :], eb[:, s, :], resid[:, t, :], ALU.add))
                link(stat(t))

            def variances(g, made, groups=GROUPS):
                tiles = slice(*groups[g:g + 2])
                nc.vector.tensor_scalar(std[:, tiles], mv[:, tiles, 1], EPS, None, ALU.add)\
                    .then_inc(made, 1)

            def normed(g, back, made, groups=GROUPS):
                tiles = slice(*groups[g:g + 2])
                dve.wait_ge(back, g + 1)
                link(nc.vector.reciprocal(rstd[:, tiles], std[:, tiles]))
                for t in range(tiles.start, tiles.stop):
                    nc.vector.tensor_scalar(resid[:, t, :], resid[:, t, :], mv[:, t, 0:1], rstd[:, t:t + 1],
                                            ALU.subtract, ALU.mult).then_inc(made, 1)

            for t in range(T + 1):
                if t < T:
                    y_of(t)
                if t >= 1:
                    z_of(t - 1)
                if t >= 4 and t % 4 == 0:
                    variances(t // 4 - 1, var_made)
                if t >= 6 and t % 4 == 2:
                    normed((t - 6) // 4, std_made, x1_made)
                if t in (12, 16):
                    copy_scores(L1, (t - 12) // 4)
            normed(3, std_made, x1_made)
            copy_scores(L1, 2)
            copy_scores(L1, 3)
            factors(L1)
            dve.wait_ge(x1_out, 16 * T)
            dve.wait_ge(x1_turned, T)
            attention(L1, "start")
            attention(L1, "units")

            def bias_residual(t):
                dve.wait_ge(x1_back[t % 2], 16 * (t // 2 + 1))
                nc.vector.tensor_tensor(resid[:, t, :], resid[:, t, :], b4_sb, ALU.add)\
                    .then_inc(res_biased, 1)

            def final(t):
                s = t % 2
                dve.wait_ge(f_ready, t + 1)
                dve.wait_ge(res_biased, t + 1)
                nc.vector.tensor_tensor(resid[:, t, :], psum[:, 7 if s else 6, :], resid[:, t, :], ALU.add)\
                    .then_inc(f_read, 1)
                dve.wait_ge(f_read, t + 1)
                link(stat(t))

            dve.wait_ge(net_in, 80)
            for c in range(4):
                if c == 1:
                    dve.wait_ge(S["l1", "hid_made"], UNITS + 1)
                if c < 3:
                    enc(c + 1)
                for t in range(4 * c, 4 * c + 4):
                    bias_residual(t)
                if c >= 2:
                    normed(c - 2, std2_made, out_made)
                if c >= 1:
                    for t in range(4 * c - 4, 4 * c):
                        final(t)
                    variances(c - 1, var2_made)
            final(12)
            normed(2, std2_made, out_made)
            final(13)
            variances(3, var2_made, GROUPS2)
            final(14)
            final(15)
            variances(4, var2_made, GROUPS2)
            normed(3, std2_made, out_made, GROUPS2)
            normed(4, std2_made, out_made, GROUPS2)

        @block.tensor
        def _(pe):
            def score_chunk(lay, c):
                i = LAYERS.index(lay)
                if c:
                    pe.wait_ge(S[lay.name, "scores_copied"], c)
                for k in range(KT):
                    last = nc.tensor.matmul(psum[0:2 * lay.H, 7, :].rearrange("p (t n) -> p t n", t=4),
                                            wa[:, i, k, 0:2 * lay.H], featT[:, 4 * c:4 * c + 4, k, :],
                                            start=(k == 0), stop=(k == KT - 1))
                last.then_inc(S[lay.name, "scores_ready"], 1)

            def turn_scores(lay):
                H = lay.H
                pe.wait_ge(S[lay.name, "scores_copied"], 4)
                for t in range(T):
                    last = nc.tensor.transpose(psum[:, 3, t * 2 * H:(t + 1) * 2 * H],
                                               scT[0:2 * H, t * P:(t + 1) * P], ident[0:2 * H, 0:2 * H])
                last.then_inc(S[lay.name, "ab_ready"], 1)

            def v_of(lay, t):
                i = LAYERS.index(lay)
                if t >= 3:
                    pe.wait_ge(S[lay.name, "v_copied"], t - 2)
                for k in range(KT):
                    last = nc.tensor.matmul(psum[:, v_bank(lay, t), :], featT[:, t, k, :],
                                            w_proj[:, i, k, :], start=(k == 0), stop=(k == KT - 1))
                last.then_inc(S[lay.name, "v_ready"], 1)

            def attention(lay):
                n = lay.name
                SB = lay.SB
                pe.wait_ge(S[n, "v_copied"], T)
                pe.wait_ge(S[n, "bmax_part_made"], 1)
                pe.sem_inc(S[n, "mask_slots_free"], MASK_SLOTS)

                def masks_wait(q, s, t):
                    pe.wait_ge(S[n, "masks_made"],
                               T * SB * q + (T * s + t + 1 + MASKS0))
                    pe.sem_inc(pe_gate, 1)

                def products(s, t, it):
                    at = slice(it * P, (it + 1) * P)
                    first = t == 0 and it % lay.per_bank == 0
                    src = pack(lay, lay.pack_slot(s))[:, t].rearrange("p m r c -> p m (r c)")
                    if t in lay.whole_tiles:
                        nc.tensor.matmul(bank_out(lay, it, 0, 2),
                                         masks(lay, t % MASK_SLOTS, 0)[:, at],
                                         src.rearrange("p m c -> p (m c)"),
                                         start=first, stop=(t == T - 1), skip_group_check=True)
                        return nc.tensor.matmul(bank_out(lay, it, 1, 2), near(lay, s, t)[:, at],
                                                src[:, 1, :], start=False, stop=(t == T - 1),
                                                skip_group_check=True)
                    for m in range(2):
                        last = nc.tensor.matmul(bank_out(lay, it, m, m + 1),
                                                masks(lay, t % MASK_SLOTS, m)[:, at], src[:, m, :],
                                                start=(first and m == 0), stop=(t == T - 1),
                                                skip_group_check=True)
                    return last

                with pe.Fori(0, lay.Q, 1) as q:
                    for s in range(SB):
                        pe.wait_ge(S[n, "lo_made"], SB * q + (lay.UH * (s // lay.UH) + FIRST_SHARES))
                        pe.sem_inc(pe_gate, 1)
                        masks_wait(q, s, BLOCK - 1)
                        for b in range(BANKS):
                            pe.wait_ge(S[n, "acc_free"], SB * BANKS * q + (BANKS * s + b + 1))
                            pe.sem_inc(pe_gate, 1)
                            for t in range(BLOCK):
                                for it in range(b * lay.per_bank, (b + 1) * lay.per_bank):
                                    last = products(s, t, it)
                        last.then_inc(S[n, "mask_slots_free"], BLOCK)
                        for t in range(BLOCK, T - BLOCK):
                            masks_wait(q, s, t)
                            for it in range(lay.NI):
                                last = products(s, t, it)
                            last.then_inc(S[n, "mask_slots_free"], 1)
                        masks_wait(q, s, T - 1)
                        for b in range(BANKS):
                            for t in range(T - BLOCK, T):
                                for it in range(b * lay.per_bank, (b + 1) * lay.per_bank):
                                    last = products(s, t, it)
                            last.then_inc(S[n, "acc_ready"], 1)

            def turn(t, bank, src):
                for k in range(KT):
                    last = nc.tensor.transpose(psum[:, bank, k * P:(k + 1) * P],
                                               src[:, t, k * P:(k + 1) * P], ident[:, :])
                return last

            pe.wait_ge(w_in[0], 16)
            pe.wait_ge(x_in[0], 16)
            v_of(L0, 0)
            v_of(L0, 1)
            pe.wait_ge(S["l0", "wa_made"], 1)
            for c in range(4):
                if c:
                    pe.wait_ge(x_in[c], 16)
                score_chunk(L0, c)
                v_of(L0, 2 + c)
            pe.wait_ge(ident_step, 2)
            turn_scores(L0)
            for t in range(6, T):
                v_of(L0, t)
            attention(L0)

            pe.wait_ge(S["l0", "acc_free"], BANKS * UNITS + 4)
            pe.wait_ge(w_in[2], 16)
            for t in range(-1, T + X1_LAG):
                if 0 <= t + 1 < T:
                    if t + 1 in (0, T // 2):
                        pe.wait_ge(S["l0", "hid_made"], UNITS + (t + 1) // (T // 2))
                    if t >= 1:
                        pe.wait_ge(h_copied, t)
                    turn(t + 1, (t + 1) % 2, feat).then_inc(h_turned, 1)
                if 0 <= t < T:
                    pe.wait_ge(h_copied, t + 1)
                    if t >= 2:
                        pe.wait_ge(y_made, t - 1)
                    for k in range(KT):
                        last = nc.tensor.matmul(psum[:, 2 + t % 2, :], hT[:, t % 2, k, :],
                                                w_proj[:, 0, k, :], start=(k == 0), stop=(k == KT - 1))
                    last.then_inc(o_ready, 1)
                if 0 <= t - 14 < 8:
                    v_of(L1, t - 14)
                if 0 <= t - X1_LAG < T:
                    pe.wait_ge(x1_made, t - X1_LAG + 1)
                    if t == X1_LAG:
                        pe.wait_ge(S["l0", "acc_free"], BANKS * UNITS + BANKS)
                    if t >= X1_LAG + 2:
                        pe.wait_ge(x1_copied, t - X1_LAG - 1)
                    turn(t - X1_LAG, 4 + (t - X1_LAG) % 2, resid).then_inc(x1_turned, 1)
                x1_tile = t - X1_LAG - 1
                if x1_tile >= 0:
                    pe.wait_ge(x1_copied, x1_tile + 1)
                    if x1_tile % 4 == 3:
                        score_chunk(L1, x1_tile // 4)
            pe.wait_ge(x1_copied, T)
            score_chunk(L1, 3)
            v_of(L1, 8)
            pe.wait_ge(y_made, T)
            turn_scores(L1)
            for t in range(9, T):
                v_of(L1, t)
            attention(L1)

            pe.wait_ge(S["l1", "acc_free"], BANKS * UNITS + 2)

            def turn_enc(t):
                pe.wait_ge(enc_made, t + 1)
                if t >= 2:
                    pe.wait_ge(e_copied, t - 1)
                turn(t, t % 2, feat).then_inc(e_turned, 1)

            def out_of(t):
                pe.wait_ge(h_made, 5 * (t // 4) + 5)
                if t >= 2:
                    pe.wait_ge(f_read, t - 1)
                for k in range(2):
                    last = nc.tensor.matmul(psum[:, 7 if t % 2 else 6, :],
                                            h3T[:, k, t % 4 * P:(t % 4 + 1) * P], w4_sb[:, k, :],
                                            start=(k == 0), stop=(k == 1))
                last.then_inc(f_ready, 1)

            def others(c, *steps):
                for what, i in steps:
                    if what is out_of and c >= 1:
                        out_of(4 * c - 4 + i)
                    if what is turn_enc and c < 3:
                        turn_enc(4 * c + 4 + i)

            for t in range(4):
                turn_enc(t)
            pe.wait_ge(S["l1", "acc_free"], BANKS * UNITS + BANKS)
            pe.wait_ge(net_in, 80)
            for c in range(4):
                pe.wait_ge(e_copied, 4 * c + 4)
                for f in range(2):
                    if c >= 1:
                        pe.wait_ge(h_made, 5 * c - 5 + f + 1)
                    for k in range(KT):
                        last = nc.tensor.matmul(psum[:, 2 + f, :], w1_sb[:, k, f * P:(f + 1) * P],
                                                encT[:, c % 2, k, :], start=(k == 0), stop=(k == KT - 1))
                    last.then_inc(h_ready, 1)
                others(c, (out_of, 0), (turn_enc, 0), (out_of, 1), (turn_enc, 1))
                pe.wait_ge(h_made, 5 * c + 2)
                for k in range(2):
                    last = nc.tensor.matmul(psum[:, 4, :], w2_sb[:, k, :], h1T[:, k, :],
                                            start=(k == 0), stop=(k == 1))
                last.then_inc(h_ready, 1)
                others(c, (turn_enc, 2), (out_of, 2), (turn_enc, 3), (out_of, 3))
                pe.wait_ge(h_made, 5 * c + 3)
                for f in range(2):
                    nc.tensor.matmul(psum[:, 4 if f else 5, :], w3_sb[:, f * P:(f + 1) * P], h2T,
                                     start=True, stop=True).then_inc(h_ready, 1)
            for t in range(12, 16):
                out_of(t)


def kernel(x, adj, L0_gnn_W_seq, L0_gnn_a1, L0_gnn_a2, L0_gnn_W_out, L0_gnn_b_out, L1_gnn_W, L1_gnn_a1,
           L1_gnn_a2, L1_gnn_W1, L1_gnn_b1, L1_gnn_W2, L1_gnn_b2, L1_gnn_W3, L1_gnn_b3, L1_gnn_W4, L1_gnn_b4):
    import numpy as np
    import concourse.bacc as bacc
    from concourse import mybir as mb
    from concourse.bass_utils import run_bass_kernel_spmd

    def flat(a, *shape):
        return np.ascontiguousarray(np.asarray(a)).reshape(*shape)

    def turned(a):
        return np.ascontiguousarray(np.asarray(a).T)

    def columns(a, n):
        return np.ascontiguousarray(np.asarray(a).reshape(n, 128).T)

    nc = bacc.Bacc("TRN2", target_bir_lowering=False, num_devices=1)
    arrays = {
        "xT": np.ascontiguousarray(np.asarray(x).reshape(T, 128, KT, 128).transpose(3, 0, 2, 1))
        .reshape(128, 4, -1),
        "x": flat(x, N, D), "adjT": turned(adj),
        "w_seq": flat(L0_gnn_W_seq, D, D), "a1_0": flat(L0_gnn_a1, 1, -1), "a2_0": flat(L0_gnn_a2, 1, -1),
        "w_out": flat(L0_gnn_W_out, D, D), "b_out": flat(L0_gnn_b_out, 1, D),
        "w_heads": np.ascontiguousarray(np.asarray(L1_gnn_W).transpose(1, 0, 2)).reshape(D, D),
        "a1_1": flat(L1_gnn_a1, 1, D), "a2_1": flat(L1_gnn_a2, 1, D),
        "w1T": turned(L1_gnn_W1), "b1": columns(L1_gnn_b1, 2),
        "w2T": turned(L1_gnn_W2), "b2": columns(L1_gnn_b2, 1),
        "w3T": turned(L1_gnn_W3), "b3": columns(L1_gnn_b3, 2),
        "w4T": turned(L1_gnn_W4), "b4": flat(L1_gnn_b4, 1, D),
    }
    args = [nc.dram_tensor(n, a.shape, mb.dt.from_np(a.dtype), kind="ExternalInput").ap()
            for n, a in arrays.items()]
    out = nc.dram_tensor("out", (T, P, D), mb.dt.float32, kind="ExternalOutput").ap()
    rows = nc.dram_tensor("rows", (16, N), mb.dt.float32).ap()
    x1_keep = nc.dram_tensor("x1_keep", (T, P, D), mb.dt.float32).ap()
    gat_kernel(nc, *args, out, rows, x1_keep)
    r = run_bass_kernel_spmd(nc, [arrays], core_ids=[0])
    return r.results[0]["out"].reshape(N, D)
```
